# Optimizing a Trainium2 kernel written in Bass

```python
import numpy as np
import jax
import jax.numpy as jnp

def _softmax(x, axis=-1):
    return jax.nn.softmax(x, axis=axis)

def _gelu(x):
    return jax.nn.gelu(x, approximate=True)

def _silu(x):
    return jax.nn.silu(x)

def _sigmoid(x):
    return jax.nn.sigmoid(x)

def _layernorm(x, axis=-1, eps=1e-05):
    m = jnp.mean(x, axis=axis, keepdims=True)
    v = jnp.var(x, axis=axis, keepdims=True)
    return (x - m) / jnp.sqrt(v + eps)

def _scatter_add(tgt, idx, src, axis=0):
    return tgt.at[idx].add(src)

def _segment_sum(src, seg, n):
    return jax.ops.segment_sum(src, seg, n)
kernel_name = 'mk_decoder_postln_d1_seqx_r8_b22e7a'

def setup_inputs(seed: int=0):
    np.random.seed(seed)
    _w = jnp.asarray

    def _rec_inputs():
        import jax
        import jax.numpy as jnp
        _rk = jax.random.key(seed)
        x = -0.0002928 + 1 * jax.random.normal(jax.random.fold_in(_rk, 1), (8, 256, 128), jnp.float32)
        _lenS = 256 - jax.random.randint(jax.random.fold_in(_rk, 7), (8,), 0, max(1, 256 // 4) + 1, jnp.int32)
        _lenS2 = 64 - jax.random.randint(jax.random.fold_in(_rk, 8), (8,), 0, max(1, 64 // 4) + 1, jnp.int32)
        _ctx_1024P = jax.random.normal(jax.random.fold_in(_rk, 11), (8, 16, 128), jnp.float32)
        _ctx_1024c = jax.random.dirichlet(jax.random.fold_in(_rk, 511), 0.3 * jnp.ones((16,), jnp.float32), (8, 64))
        _ctx_1024t = jnp.einsum('bsk,bkd->bsd', _ctx_1024c, _ctx_1024P)
        _ctx_1024t = _ctx_1024t * jax.lax.rsqrt(jnp.mean(jnp.square(_ctx_1024t)) + 1e-12) * 0.953939
        ctx_1024 = -1.39393e-06 + 0.999914 * (_ctx_1024t + 0.3 * jax.random.normal(jax.random.fold_in(_rk, 611), (8, 64, 128), jnp.float32))
        _validS = jnp.arange(256)[None, :] < _lenS[:, None]
        _validS2 = jnp.arange(64)[None, :] < _lenS2[:, None]
        _causal = jnp.tril(jnp.ones((256, 256), dtype=bool))
        mask_1x1xSxS2_fk1 = jnp.where(jnp.broadcast_to(_validS2[0:1, None, None, :], (1, 1, 256, 64)), 1.0, 0.0).astype(jnp.float32)
        return (x, ctx_1024, mask_1x1xSxS2_fk1)
    x, ctx_1024, mask_1x1xSxS2_fk1 = _rec_inputs()

    def _L0_attn_setup():
        import jax, jax.numpy as jnp
        import numpy as np
        B, S, D = (2, 256, 128)
        H = 16
        HD = D // H

        def _rope_tables(seq_len, head_dim, dtype):
            pos = jnp.arange(seq_len, dtype=dtype)
            inv = jnp.power(10000.0, -2.0 * jnp.arange(head_dim // 2, dtype=dtype) / head_dim)
            ang = pos[:, None] * inv[None, :]
            cos_pos = jnp.repeat(jnp.cos(ang), 2, axis=-1)
            sin_pos = jnp.repeat(jnp.sin(ang), 2, axis=-1)
            return (cos_pos, sin_pos)

        def _rotate_half_interleaved(x):
            x2 = jnp.stack([-x[..., 1::2], x[..., 0::2]], axis=-1)
            return x2.reshape(x.shape)
        key = jax.random.key(seed)
        ks = jax.random.split(key, 4)
        scale = 1.0 / np.sqrt(D)
        return {'hidden_states': jax.random.normal(ks[0], (B, S, D), jnp.float32), 'Wq': jax.random.normal(ks[1], (D, D), jnp.float32) * scale, 'bq': jnp.zeros((D,), jnp.float32), 'Wk': jax.random.normal(ks[2], (D, D), jnp.float32) * scale, 'bk': jnp.zeros((D,), jnp.float32), 'Wv': jax.random.normal(ks[3], (D, D), jnp.float32) * scale, 'bv': jnp.zeros((D,), jnp.float32)}
    _L0_attn_all = _L0_attn_setup()
    _L0_attn_in = {k: v for k, v in _L0_attn_all.items() if k in ('Wq', 'bq', 'Wk', 'bk', 'Wv', 'bv')}
    del _L0_attn_all

    def _L0_xattn_setup():
        import jax, jax.numpy as jnp
        import numpy as np
        B, S, D, H = (2, 256, 128, 16)
        DEPTH = D // H

        def _split_heads(x):
            b, s, _ = x.shape
            return x.reshape(b, s, H, DEPTH).transpose(0, 2, 1, 3)
        key = jax.random.key(seed)
        ks = jax.random.split(key, 12)
        scale = 1.0 / np.sqrt(D)
        inp = {'query': jax.random.normal(ks[0], (B, S, D), jnp.float32), 'key_': jax.random.normal(ks[1], (B, S, D), jnp.float32), 'value': jax.random.normal(ks[2], (B, S, D), jnp.float32), 'mask': jnp.triu(jnp.ones((S, S), jnp.float32), k=1)[None, None], 'wq_w': jax.random.normal(ks[3], (D, D), jnp.float32) * scale, 'wq_b': jnp.zeros((D,), jnp.float32), 'wk_w': jax.random.normal(ks[4], (D, D), jnp.float32) * scale, 'wk_b': jnp.zeros((D,), jnp.float32), 'wv_w': jax.random.normal(ks[5], (D, D), jnp.float32) * scale, 'wv_b': jnp.zeros((D,), jnp.float32), 'dense_w': jax.random.normal(ks[6], (D, D), jnp.float32) * scale, 'dense_b': jnp.zeros((D,), jnp.float32)}
        return inp
    _L0_xattn_all = _L0_xattn_setup()
    _L0_xattn_in = {k: v for k, v in _L0_xattn_all.items() if k in ('wq_w', 'wq_b', 'wk_w', 'wk_b', 'wv_w', 'wv_b', 'dense_w', 'dense_b')}
    del _L0_xattn_all

    def _L0_ffn_setup():
        import jax, jax.numpy as jnp
        import numpy as np
        HIDDEN = 128
        INTER = 512
        key = jax.random.key(seed)
        k1, k2, k3, k4, k5 = jax.random.split(key, 5)
        hidden_states = jax.random.normal(k1, (4, 256, HIDDEN), dtype=jnp.float32)
        W1 = jax.random.normal(k2, (HIDDEN, INTER), dtype=jnp.float32) * (1.0 / np.sqrt(HIDDEN))
        b1 = jax.random.normal(k3, (INTER,), dtype=jnp.float32) * 0.02
        W2 = jax.random.normal(k4, (INTER, HIDDEN), dtype=jnp.float32) * (1.0 / np.sqrt(INTER))
        b2 = jax.random.normal(k5, (HIDDEN,), dtype=jnp.float32) * 0.02
        return {'hidden_states': hidden_states, 'W1': W1, 'b1': b1, 'W2': W2, 'b2': b2}
    _L0_ffn_all = _L0_ffn_setup()
    _L0_ffn_in = {k: v for k, v in _L0_ffn_all.items() if k in ('W1', 'b1', 'W2', 'b2')}
    del _L0_ffn_all
    return {'x': x, 'ctx_1024': ctx_1024, 'mask_1x1xSxS2_fk1': mask_1x1xSxS2_fk1, 'L0_attn_Wq': _L0_attn_in['Wq'], 'L0_attn_bq': _L0_attn_in['bq'], 'L0_attn_Wk': _L0_attn_in['Wk'], 'L0_attn_bk': _L0_attn_in['bk'], 'L0_attn_Wv': _L0_attn_in['Wv'], 'L0_attn_bv': _L0_attn_in['bv'], 'L0_xattn_wq_w': _L0_xattn_in['wq_w'], 'L0_xattn_wq_b': _L0_xattn_in['wq_b'], 'L0_xattn_wk_w': _L0_xattn_in['wk_w'], 'L0_xattn_wk_b': _L0_xattn_in['wk_b'], 'L0_xattn_wv_w': _L0_xattn_in['wv_w'], 'L0_xattn_wv_b': _L0_xattn_in['wv_b'], 'L0_xattn_dense_w': _L0_xattn_in['dense_w'], 'L0_xattn_dense_b': _L0_xattn_in['dense_b'], 'L0_ffn_W1': _L0_ffn_in['W1'], 'L0_ffn_b1': _L0_ffn_in['b1'], 'L0_ffn_W2': _L0_ffn_in['W2'], 'L0_ffn_b2': _L0_ffn_in['b2']}

def reference(x, ctx_1024, mask_1x1xSxS2_fk1, L0_attn_Wq, L0_attn_bq, L0_attn_Wk, L0_attn_bk, L0_attn_Wv, L0_attn_bv, L0_xattn_wq_w, L0_xattn_wq_b, L0_xattn_wk_w, L0_xattn_wk_b, L0_xattn_wv_w, L0_xattn_wv_b, L0_xattn_dense_w, L0_xattn_dense_b, L0_ffn_W1, L0_ffn_b1, L0_ffn_W2, L0_ffn_b2):
    import jax
    import jax.numpy as jnp

    def _L0_attn_ref(hidden_states, Wq, bq, Wk, bk, Wv, bv):
        import jax, jax.numpy as jnp
        import numpy as np
        B, S, D = (2, 256, 128)
        H = 16
        HD = D // H

        def _rope_tables(seq_len, head_dim, dtype):
            pos = jnp.arange(seq_len, dtype=dtype)
            inv = jnp.power(10000.0, -2.0 * jnp.arange(head_dim // 2, dtype=dtype) / head_dim)
            ang = pos[:, None] * inv[None, :]
            cos_pos = jnp.repeat(jnp.cos(ang), 2, axis=-1)
            sin_pos = jnp.repeat(jnp.sin(ang), 2, axis=-1)
            return (cos_pos, sin_pos)

        def _rotate_half_interleaved(x):
            x2 = jnp.stack([-x[..., 1::2], x[..., 0::2]], axis=-1)
            return x2.reshape(x.shape)
        b, s, d = hidden_states.shape
        q = hidden_states @ Wq + bq
        k = hidden_states @ Wk + bk
        v = hidden_states @ Wv + bv
        q = q.reshape(b, s, H, HD).transpose(0, 2, 1, 3)
        k = k.reshape(b, s, H, HD).transpose(0, 2, 1, 3)
        v = v.reshape(b, s, H, HD).transpose(0, 2, 1, 3)
        cos_pos, sin_pos = _rope_tables(s, HD, hidden_states.dtype)
        q = q * cos_pos + _rotate_half_interleaved(q) * sin_pos
        k = k * cos_pos + _rotate_half_interleaved(k) * sin_pos
        scores = jnp.einsum('bhqd,bhkd->bhqk', q, k) / jnp.sqrt(jnp.asarray(HD, hidden_states.dtype))
        probs = jax.nn.softmax(scores, axis=-1)
        ctx = jnp.einsum('bhqk,bhkd->bhqd', probs, v)
        ctx = ctx.transpose(0, 2, 1, 3).reshape(b, s, d)
        return ctx

    def _L0_xattn_ref(query, key_, value, mask, wq_w, wq_b, wk_w, wk_b, wv_w, wv_b, dense_w, dense_b):
        import jax, jax.numpy as jnp
        import numpy as np
        B, S, D, H = (2, 256, 128, 16)
        DEPTH = D // H

        def _split_heads(x):
            b, s, _ = x.shape
            return x.reshape(b, s, H, DEPTH).transpose(0, 2, 1, 3)
        q = _split_heads(query @ wq_w.T + wq_b)
        k = _split_heads(key_ @ wk_w.T + wk_b)
        v = _split_heads(value @ wv_w.T + wv_b)
        logits = jnp.einsum('bhqd,bhkd->bhqk', q, k) / jnp.sqrt(jnp.float32(DEPTH))
        logits = logits + mask * -1000000000.0
        attn = jax.nn.softmax(logits, axis=-1)
        out = jnp.einsum('bhqk,bhkd->bhqd', attn, v)
        out = out.transpose(0, 2, 1, 3).reshape(query.shape[0], -1, D)
        return out @ dense_w.T + dense_b

    def _L0_ffn_ref(hidden_states, W1, b1, W2, b2):
        import jax, jax.numpy as jnp
        import numpy as np
        HIDDEN = 128
        INTER = 512
        h = jax.nn.relu(jnp.einsum('bsh,hi->bsi', hidden_states, W1) + b1)
        return jnp.einsum('bsi,ih->bsh', h, W2) + b2
    x = _layernorm(x + _L0_attn_ref(x, L0_attn_Wq, L0_attn_bq, L0_attn_Wk, L0_attn_bk, L0_attn_Wv, L0_attn_bv), axis=-1)
    x = _layernorm(x + _L0_xattn_ref(x, ctx_1024, ctx_1024, mask_1x1xSxS2_fk1, L0_xattn_wq_w, L0_xattn_wq_b, L0_xattn_wk_w, L0_xattn_wk_b, L0_xattn_wv_w, L0_xattn_wv_b, L0_xattn_dense_w, L0_xattn_dense_b), axis=-1)
    x = _layernorm(x + _L0_ffn_ref(x, L0_ffn_W1, L0_ffn_b1, L0_ffn_W2, L0_ffn_b2), axis=-1)
    return x

_drawn_inputs = setup_inputs


def setup_inputs(seed=0):
    import zlib

    import numpy as np

    out = dict(_drawn_inputs(seed))
    spreads = {'L0_attn_bq': (0.0, 0.8),
     'L0_attn_bk': (0.0, 0.8),
     'L0_attn_bv': (0.0, 0.1),
     'L0_xattn_wq_b': (0.0, 0.339),
     'L0_xattn_wk_b': (0.0, 0.8),
     'L0_xattn_wv_b': (0.0, 0.1),
     'L0_xattn_dense_b': (0.0, 0.1)}
    factors = {'L0_ffn_b1': 5.121, 'L0_ffn_b2': 3.43}
    for name, (base, spread) in spreads.items():
        noise = np.random.default_rng([zlib.crc32(name.encode()), seed]).standard_normal(out[name].shape)
        drawn = base * np.exp(spread * noise) if base else spread * noise
        out[name] = jnp.asarray(drawn.astype(out[name].dtype))
    for name, factor in factors.items():
        out[name] = (out[name] * factor).astype(out[name].dtype)
    return out
```

```python
from contextlib import ExitStack

import concourse.bass as bass
from concourse import mybir

F32 = mybir.dt.float32
F32R = mybir.dt.float32r
ALU = mybir.AluOpType
ACT = mybir.ActivationFunctionType
AX = mybir.AxisListType

P = 128
B, S, D = 8, 256, 128
SC = 64
H, HD = 16, 8
FF = 512
QT = S // P
QUADS, HQ = 4, 4
PAIRS = H // 2
FC = FF // P
STRIP = 32
QROWS = HQ * HD
NROWS = 3 * QROWS
MROWS = 2 * HQ
EPS = 1e-5
MASK_SCALE = -1e9
KSCALE = HD ** -0.5

FIRST = [("ident", P), ("wq", D), ("wk", D), ("wv", D), ("bq", 1), ("bk", 1), ("cos", 2 * S), ("sin", 2 * S),
         ("head_of_row", HQ), ("bv", D)]
LATER = [("wqx", D), ("wkx", D), ("wvx", D), ("dense", D), ("w1", FF), ("w2", FC * D), ("bqx", 1), ("bkx", 1),
         ("b1", FC), ("bvx", D), ("dense_b", D), ("b2", D), ("mask", S), ("key_of_row", 8 * SC)]


def columns(fields):
    at, n = {}, 0
    for name, width in fields:
        at[name] = (n, width)
        n += width
    return at, n


FIRST_AT, FIRST_N = columns(FIRST)
LATER_AT, LATER_N = columns(LATER)


def build(nc, x_d, ctx_d, first_d, later_d, out_d):
    with ExitStack() as ctx:
        def sb(name, shape):
            return ctx.enter_context(nc.sbuf_tensor(name, shape, F32))

        def psum(name, shape):
            return ctx.enter_context(nc.psum_tensor(name, shape, F32))

        def sem(name):
            return ctx.enter_context(nc.semaphore(name))

        def sems(name, n):
            return [sem(f"{name}{j}") for j in range(n)]

        qx_scratch = nc.dram_tensor("qx_scratch", [P, 2, S], F32, kind="Internal").ap()
        kx_scratch = nc.dram_tensor("kx_scratch", [P, 2, SC], F32, kind="Internal").ap()

        first = sb("first_sb", [P, FIRST_N])
        later = sb("later_sb", [P, LATER_N])

        def c1(name):
            a, w = FIRST_AT[name]
            return first[:, a:a + w]

        def c2(name):
            a, w = LATER_AT[name]
            return later[:, a:a + w]

        x_in = sb("x_in", [P, QT, D])
        x_res = sb("x_res", [P, QT, D])
        ctx_in = sb("ctx_in", [P, D])
        xT = sb("xT", [P, S])
        qk = sb("qk", [P, 2, S])
        qk_swapped = sb("qk_swapped", [P, 2, S])
        qk_cos = sb("qk_cos", [P, 2, S])
        qk_sin = sb("qk_sin", [P, 2, S])
        qk_rope = sb("qk_rope", [P, 2, S])
        qk_parts = sb("qk_parts", [P, 4, S])
        slots = sb("slots", [P, QUADS, 2, S])
        k_diag = sb("k_diag", [P, QUADS, HQ, S])
        v_rows = sb("v_rows", [P, QT, D])
        v_ones = sb("v_ones", [P, QT, H, STRIP])
        neg_max = sb("neg_max", [P, QUADS, QT, HQ])
        max_parts = sb("max_parts", [P, QUADS, QT, MROWS])
        probs = sb("probs", [P, 2, HQ, QT, S])
        ctxvT = sb("ctxvT", [P, QUADS, S])
        recip1 = sb("recip1", [P, QT * H])
        att1 = sb("att1", [P, QT, D])
        sum1 = sb("sum1", [P, QT, D])
        x1 = sb("x1", [P, QT, D])
        x1_bias = sb("x1_bias", [P, QT, D])
        x1T = sb("x1T", [P, S])
        qx = sb("qx", [P, S])
        qx_parts = sb("qx_parts", [P, 2, S])
        qx_slots = sb("qx_slots", [P, QUADS, S])
        ctxT2 = sb("ctxT2", [P, 2 * SC])
        kx = sb("kx", [P, SC])
        kx_parts = sb("kx_parts", [P, 2, SC])
        kx_slots = sb("kx_slots", [P, QUADS, SC])
        kx_diag = sb("kx_diag", [P, QUADS, HQ, SC])
        vx_ones = sb("vx_ones", [P, PAIRS, STRIP])
        neg_maxx = sb("neg_maxx", [P, QT * QUADS, HQ])
        maxx_parts = sb("maxx_parts", [P, QT * QUADS, STRIP])
        probsx = sb("probsx", [P, PAIRS, S])
        attvT = sb("attvT", [P, 2, S])
        recip2 = sb("recip2", [P, QT * H])
        att2 = sb("att2", [P, QT, D])
        att2T = sb("att2T", [P, S])
        sum2 = sb("sum2", [P, QT, D])
        x2 = sb("x2", [P, QT, D])
        x2_bias = sb("x2_bias", [P, QT, D])
        x2T = sb("x2T", [P, S])
        hT = sb("hT", [P, FC, S])
        sum3 = sb("sum3", [P, QT, D])
        y = sb("y", [P, QT, D])
        stats = sb("stats", [P, 3, QT, 6])
        mean_var = sb("mean_var", [P, 3, QT, 2])
        var_eps = sb("var_eps", [P, 3, QT])
        rstd = sb("rstd", [P, 3, QT])
        minus_half = sb("minus_half", [P, QT])
        mask_neg = sb("mask_neg", [P, S])
        mask_parts = sb("mask_parts", [P, S])
        mask_hi = sb("mask_hi", [P, S])
        key_of_row = sb("key_of_row", [P, 8 * SC])

        scores_qk = psum("scores_qk", [P, 1024])
        scores_kq = psum("scores_kq", [P, 1024])
        pv_acc = psum("pv_acc", [P, 2, S])
        prep_ps = psum("prep_ps", [P, 512])
        tail_ps = psum("tail_ps", [P, 2, 512])

        first_in, later_in, zeroed, consts_ready = sem("first_in"), sem("later_in"), sem("zeroed"), sem("consts_ready")
        mask_step = sem("mask_step")
        x_loaded, xres_loaded, ctx_loaded = sem("x_loaded"), sem("xres_loaded"), sem("ctx_loaded")
        xT_made, xT_copied = sem("xT_made"), sem("xT_copied")
        qk_made, qk_copied, qk_swap_in = sem("qk_made"), sem("qk_copied"), sem("qk_swap_in")
        rope_cos, rope_sin, rope_done = sem("rope_cos"), sem("rope_sin"), sem("rope_done")
        qk_hi_done, qk_lo_done = sem("qk_hi_done"), sem("qk_lo_done")
        v_made, v_copied, v_placed = sem("v_made"), sem("v_copied"), sem("v_placed")
        slots_in, diag_done = sems("slots_in", QUADS), sems("diag_done", QUADS)
        max_ready = [sems(f"max_ready{g}_", QT) for g in range(QUADS)]
        max_done = [sems(f"max_done{g}_", QT) for g in range(QUADS)]
        max_hi_done, max_split = sems("max_hi_done", QUADS), sems("max_split", QUADS)
        maxT_made, maxT_in = sems("maxT_made", QUADS), sems("maxT_in", QUADS)
        exp_ready = [sems(f"exp_ready{g}_", 2) for g in range(QUADS)]
        exp_done = [sems(f"exp_done{g}_", 2) for g in range(QUADS)]
        pv_done = sems("pv_done", QUADS)
        pv_copied = sems("pv_copied", 2)
        pvT_made = sem("pvT_made")
        recip1_done, att1_done, sum1_done = sem("recip1_done"), sem("att1_done"), sem("sum1_done")
        stats_done, aggr_done, var_done, rstd_done = (sems(n, 3) for n in ("stats_done", "aggr_done", "var_done", "rstd_done"))
        x1_done, x1b_done, x1T_made, x1T_copied = sem("x1_done"), sem("x1b_done"), sem("x1T_made"), sem("x1T_copied")
        qx_made, qx_copied, qx_hi_done, qx_lo_done = sem("qx_made"), sem("qx_copied"), sem("qx_hi_done"), sem("qx_lo_done")
        qx_out, qx_slots_in = sem("qx_out"), sem("qx_slots_in")
        ctxT_made, ctxT_copied = sem("ctxT_made"), sem("ctxT_copied")
        kvx_made, kx_copied, vx_copied = sem("kvx_made"), sem("kx_copied"), sem("vx_copied")
        kx_hi_done, kx_lo_done, kx_out, kx_slots_in = sem("kx_hi_done"), sem("kx_lo_done"), sem("kx_out"), sem("kx_slots_in")
        kx_diag_done = sem("kx_diag_done")
        maxx_ready, maxx_done = sems("maxx_ready", QT), sems("maxx_done", QT)
        maxx_hi_done, maxx_split, maxxT_made, maxxT_in = sem("maxx_hi_done"), sem("maxx_split"), sem("maxxT_made"), sem("maxxT_in")
        expx_ready, expx_done = sems("expx_ready", 2), sems("expx_done", 2)
        pvx_done, pvx_copied, pvxT_made = sem("pvx_done"), sem("pvx_copied"), sem("pvxT_made")
        recip2_done, att2_done, att2T_made, att2T_copied = sem("recip2_done"), sem("att2_done"), sem("att2T_made"), sem("att2T_copied")
        dense_made, sum2_done, x2_done, x2b_done = sem("dense_made"), sem("sum2_done"), sem("x2_done"), sem("x2b_done")
        x2T_made, x2T_copied, h_made, h_copied = sem("x2T_made"), sem("x2T_copied"), sem("h_made"), sem("h_copied")
        ffn_made, sum3_done, y_done, stored = sem("ffn_made"), sem("sum3_done"), sem("y_done"), sem("stored")

        def fixed_wait(eng):
            eng.wait_ge(first_in, 16)

        FIRST_LOOPED, END_LOOPED = 3, B - 2

        class Counts:

            def __init__(self, at):
                self.n, self.s, self.m, self.t, self.t1 = (
                    at("n", 2, 1), at("s", 1, 1), at("m", 0, 1), at("t", -1, 1), at("t1", -2, 1))

            def dma(self, at):
                self.n_16, self.n_32, self.n_48 = at("n16", 2, 16), at("n32", 2, 32), at("n48", 2, 48)
                self.s_32, self.s_48 = at("s32", 1, 32), at("s48", 1, 48)
                self.m_16, self.m_32, self.m_48 = at("m16", 0, 16), at("m32", 0, 32), at("m48", 0, 48)
                self.t_16, self.t_48, self.t1_16 = at("t16", -1, 16), at("t48", -1, 48), at("t1_16", -2, 16)
                return self

        def peeled(e):
            number = lambda name, k, unit: min(max(0, e + k), B) * unit
            r = Counts(number).dma(number)
            r.e = e
            r.prep, r.self_, r.mid, r.tail, r.load = e + 1 < B, 0 <= e < B, 0 <= e - 1 < B, 0 <= e - 2 < B, e + 2 < B
            return r

        def iterations(eng, name, body):
            for e in range(-1, FIRST_LOOPED):
                body(peeled(e))
            registers = []

            def register(role, k, unit):
                reg = eng.alloc_register(f"{name}_{role}_runs")
                eng.reg_mov(reg, (FIRST_LOOPED + k) * unit)
                registers.append((reg, unit))
                return reg

            r = Counts(register).dma(register)
            r.prep = r.self_ = r.mid = r.tail = r.load = True
            with eng.Fori(FIRST_LOOPED, END_LOOPED) as e:
                r.e = e
                body(r)
                for reg, unit in registers:
                    eng.reg_add(reg, reg, unit)
            for e in range(END_LOOPED, B + 2):
                body(peeled(e))

        block = ctx.enter_context(nc.Block())

        @block.sync
        def _(sp):
            sp.dma_start(x_in[:], x_d[0].rearrange("(t p) d -> p t d", p=P)).then_inc(x_loaded, 16)
            sp.dma_start(first[:], first_d).then_inc(first_in, 16)
            sp.dma_start(later[:], later_d).then_inc(later_in, 16)

            def slot_loads(g, made, used):
                sp.wait_ge(qk_lo_done, made)
                if used:
                    sp.wait_ge(exp_ready[g][1], used)
                if used:
                    sp.wait_ge(diag_done[g], used)
                for s, (qp, kp) in enumerate(((0, 2), (0, 3), (1, 2))):
                    sp.dma_start(slots[QROWS * s:QROWS * (s + 1), g, :, :],
                                 qk_parts[QROWS * g:QROWS * (g + 1), qp:kp + 1:kp - qp, :]).then_inc(slots_in[g], 16)

            def body(r):
                if r.mid:
                    fixed_wait(sp)
                    if r.t:
                        sp.wait_ge(sum1_done, r.t)
                    sp.dma_start(x_res[:], x_d[r.e - 1].rearrange("(t p) d -> p t d", p=P)).then_inc(xres_loaded, 16)
                    fixed_wait(sp)
                    if r.t:
                        sp.wait_ge(ctxT_made, r.t)
                    for j in range(2):
                        sp.dma_start(ctx_in[j * SC:(j + 1) * SC, :], ctx_d[r.e - 1]).then_inc(ctx_loaded, 16)
                if r.prep:
                    sp.wait_ge(qk_copied, r.n)
                    if r.s:
                        sp.wait_ge(rope_sin, r.s)
                    for half in range(2):
                        sp.dma_start(qk_swapped[half:P:2, :, :], qk[1 - half:P:2, :, :]).then_inc(qk_swap_in, 16)
                if r.load:
                    fixed_wait(sp)
                    if r.n:
                        sp.wait_ge(xT_made, r.n)
                    sp.dma_start(x_in[:], x_d[r.e + 2].rearrange("(t p) d -> p t d", p=P)).then_inc(x_loaded, 16)
                if r.prep:
                    slot_loads(0, r.n, r.s)
                if r.mid:
                    sp.wait_ge(qx_lo_done, r.m)
                    if r.t:
                        sp.wait_ge(qx_slots_in, r.t_48)
                    sp.dma_start(qx_scratch, qx_parts[:]).then_inc(qx_out, 16)
                if r.prep:
                    slot_loads(1, r.n, r.s)
                if r.mid:
                    sp.wait_ge(qx_out, r.m_16)
                    if r.t:
                        sp.wait_ge(expx_ready[1], r.t)
                    for s, part in enumerate((0, 0, 1)):
                        sp.dma_start(qx_slots[QROWS * s:QROWS * (s + 1), :, :],
                                     qx_scratch[:, part, :].rearrange("(g r) c -> r g c", g=QUADS)).then_inc(qx_slots_in, 16)
                if r.prep:
                    slot_loads(2, r.n, r.s)
                if r.mid:
                    sp.wait_ge(kx_lo_done, r.m)
                    if r.t:
                        sp.wait_ge(kx_slots_in, r.t_48)
                    sp.dma_start(kx_scratch, kx_parts[:]).then_inc(kx_out, 16)
                    sp.wait_ge(kx_out, r.m_16)
                    if r.t:
                        sp.wait_ge(kx_diag_done, r.t)
                    for s, part in enumerate((0, 1, 0)):
                        sp.dma_start(kx_slots[QROWS * s:QROWS * (s + 1), :, :],
                                     kx_scratch[:, part, :].rearrange("(g r) c -> r g c", g=QUADS)).then_inc(kx_slots_in, 16)
                if r.prep:
                    slot_loads(3, r.n, r.s)
                if r.tail:
                    fixed_wait(sp)
                    sp.wait_ge(y_done, r.t)
                    sp.dma_start(out_d[r.e - 2].rearrange("(t p) d -> p t d", p=P), y[:]).then_inc(stored, 16)

            iterations(sp, "sp", body)
            sp.wait_ge(stored, 16 * B)

        @block.tensor
        def _(pe):
            ident = c1("ident")
            sp_r, kd_r = slots[:].bitcast(F32R), k_diag[:].bitcast(F32R)
            qxs_r, kxd_r = qx_slots[:].bitcast(F32R), kx_diag[:].bitcast(F32R)
            mask_r, keys_r = mask_parts[:].bitcast(F32R), key_of_row[:].bitcast(F32R)

            def max_scores(g, t, done, free, free_count):
                pe.wait_ge(diag_done[g], done)
                if free_count:
                    pe.wait_ge(free, free_count)
                for h in range(0, HQ, 2):
                    mm = pe.matmul(scores_qk[:, h * S:(h + 2) * S], sp_r[0:NROWS, g, 0, t * P:(t + 1) * P],
                                   kd_r[0:NROWS, g, h:h + 2, :], start=True, stop=True)
                mm.then_inc(max_ready[g][t], 1)

            def exp_scores(g, half, done, free, free_count):
                if half == 0:
                    pe.wait_ge(maxT_in[g], done)
                if free_count:
                    pe.wait_ge(free, free_count)
                for j in range(2):
                    for kt in range(QT):
                        mm = pe.matmul(scores_kq[:, (2 * j + kt) * S:(2 * j + kt + 1) * S],
                                       kd_r[:, g, 2 * half + j, kt * P:(kt + 1) * P], sp_r[:, g, 0, :],
                                       start=True, stop=True)
                mm.then_inc(exp_ready[g][half], 1)

            def max_transposes(g, done):
                pe.wait_ge(max_split[g], done)
                for t in range(QT):
                    mm = pe.transpose(prep_ps[0:MROWS, t * P:(t + 1) * P], max_parts[:, g, t, :], ident)
                mm.then_inc(maxT_made[g], 1)

            def pv(g, done, previous):
                pe.wait_ge(exp_done[g][0], done)
                pe.wait_ge(exp_done[g][1], done)
                if g == 0:
                    pe.wait_ge(v_placed, done)
                    if previous:
                        pe.wait_ge(pv_copied[1], previous)
                if g == 2:
                    pe.wait_ge(pv_copied[0], done)
                for kt in range(QT):
                    for h in range(HQ):
                        mm = pe.matmul(pv_acc[STRIP * h:STRIP * (h + 1), g % 2, :], v_ones[:, kt, HQ * g + h, :],
                                       probs[:, g % 2, h, kt, :], start=(kt == 0), stop=(kt == QT - 1),
                                       tile_position=(0, STRIP * h))
                mm.then_inc(pv_done[g], 1)

            def maxx_scores(t, r):
                if t == 0:
                    if r.t:
                        pe.wait_ge(kx_diag_done, r.t)
                    if r.t:
                        pe.wait_ge(qx_slots_in, r.t_48)
                    if r.self_:
                        pe.wait_ge(max_done[1][1], r.s)
                    else:
                        pe.wait_ge(max_done[3][1], B)
                        if r.t1:
                            pe.wait_ge(maxx_done[1], r.t1)
                else:
                    if r.t:
                        pe.wait_ge(maxx_done[0], r.t)
                for half in range(2):
                    pe.matmul(scores_qk[:, half * 512:(half + 1) * 512], mask_r[:, t * P:(t + 1) * P], keys_r,
                              start=True, stop=False, skip_group_check=True)
                    for g in range(2 * half, 2 * half + 2):
                        mm = pe.matmul(scores_qk[:, g * 256:(g + 1) * 256], qxs_r[0:NROWS, g, t * P:(t + 1) * P],
                                       kxd_r[0:NROWS, g, :, :], start=False, stop=True, skip_group_check=True)
                mm.then_inc(maxx_ready[t], 1)

            def expx_scores(u, r):
                if u == 0:
                    if r.t:
                        pe.wait_ge(maxxT_in, r.t)
                    if r.self_:
                        pe.wait_ge(exp_done[1][1], r.s)
                    else:
                        pe.wait_ge(exp_done[3][1], B)
                        if r.t1:
                            pe.wait_ge(expx_done[1], r.t1)
                else:
                    if r.t:
                        pe.wait_ge(expx_done[0], r.t)
                for p in range(4 * u, 4 * u + 4):
                    o = scores_kq[:, (p % 4) * S:(p % 4 + 1) * S]
                    pe.matmul(o, keys_r[:, 0:P], mask_r, start=True, stop=False)
                    mm = pe.matmul(o, kxd_r[:, p // 2, 2 * (p % 2):2 * (p % 2) + 2, :], qxs_r[:, p // 2, :],
                                   start=False, stop=True)
                mm.then_inc(expx_ready[u], 1)

            def body(r):
                if r.self_:
                    max_scores(1, 0, r.s, max_done[0][1], r.s)
                    exp_scores(0, 0, r.s, exp_done[3][1], r.m)
                if r.prep:
                    if not r.self_:
                        pe.wait_ge(first_in, 16)
                    pe.wait_ge(x_loaded, r.n_16)
                    for t in range(QT):
                        mm = pe.transpose(prep_ps[:, t * P:(t + 1) * P], x_in[:, t, :], ident)
                    mm.then_inc(xT_made, 1)
                if r.self_:
                    max_scores(1, 1, r.s, max_done[1][0], r.s)
                if r.mid:
                    pv(3, r.m, r.t)
                if r.prep:
                    pe.wait_ge(xT_copied, r.n)
                    pe.matmul(prep_ps[:, 0:S], c1("wq"), xT[:], start=True, stop=True)
                    pe.matmul(prep_ps[:, S:2 * S], c1("wk"), xT[:], start=True, stop=True).then_inc(qk_made, 1)
                if r.self_:
                    exp_scores(0, 1, r.s, exp_done[0][0], r.s)
                if r.tail:
                    maxx_scores(0, r)
                if r.mid:
                    pe.wait_ge(pv_copied[1], r.m)
                    if r.t1:
                        pe.wait_ge(sum3_done, r.t1)
                    for t in range(QT):
                        for g in range(QUADS):
                            mm = pe.transpose(tail_ps[:, t, g * P:(g + 1) * P], ctxvT[:, g, t * P:(t + 1) * P], ident)
                    mm.then_inc(pvT_made, 1)
                if r.self_:
                    if r.prep:
                        pe.wait_ge(qk_copied, r.n)
                    max_transposes(1, r.s)
                if r.tail:
                    maxx_scores(1, r)
                if r.self_:
                    if r.t:
                        pe.wait_ge(maxx_done[1], r.t)
                    max_scores(2, 0, r.s, max_done[1][1], r.s)
                    exp_scores(1, 0, r.s, exp_done[0][1], r.s)
                if r.prep:
                    pe.wait_ge(qk_copied, r.n)
                    for t in range(QT):
                        mm = pe.matmul(prep_ps[:, t * P:(t + 1) * P], xT[:, t * P:(t + 1) * P], c1("wv"),
                                       start=True, stop=True)
                    mm.then_inc(v_made, 1)
                if r.self_:
                    max_scores(2, 1, r.s, max_done[2][0], r.s)
                    pv(0, r.s, r.m)
                if r.tail:
                    if r.prep:
                        pe.wait_ge(v_copied, r.n)
                    pe.wait_ge(vx_copied, r.t)
                    pe.wait_ge(maxx_split, r.t)
                    for t in range(QT):
                        mm = pe.transpose(prep_ps[:, t * P:(t + 1) * P],
                                          maxx_parts[:, t * QUADS:(t + 1) * QUADS, :], ident)
                    mm.then_inc(maxxT_made, 1)
                if r.mid:
                    pe.wait_ge(x1_done, r.m)
                    for t in range(QT):
                        mm = pe.transpose(tail_ps[:, 0, t * P:(t + 1) * P], x1[:, t, :], ident)
                    mm.then_inc(x1T_made, 1)
                if r.self_:
                    exp_scores(1, 1, r.s, exp_done[1][0], r.s)
                    if r.prep:
                        pe.wait_ge(v_copied, r.n)
                    if r.t:
                        pe.wait_ge(maxxT_in, r.t)
                    max_transposes(2, r.s)
                if r.tail:
                    expx_scores(0, r)
                if r.mid:
                    pe.wait_ge(x1T_copied, r.m)
                    pe.matmul(tail_ps[:, 1, 0:S], c2("wqx"), x1T[:], start=True, stop=True).then_inc(qx_made, 1)
                if r.self_:
                    max_scores(3, 0, r.s, max_done[2][1], r.s)
                if r.tail:
                    expx_scores(1, r)
                if r.self_:
                    if r.t:
                        pe.wait_ge(expx_done[1], r.t)
                    exp_scores(2, 0, r.s, exp_done[1][1], r.s)
                if r.mid:
                    if r.t:
                        pe.wait_ge(maxxT_in, r.t)
                    pe.wait_ge(ctx_loaded, r.m_32)
                    pe.transpose(prep_ps[:, 0:P], ctx_in[:], ident).then_inc(ctxT_made, 1)
                if r.self_:
                    max_scores(3, 1, r.s, max_done[3][0], r.s)
                    pv(1, r.s, r.m)
                if r.tail:
                    pe.wait_ge(expx_done[0], r.t)
                    pe.wait_ge(expx_done[1], r.t)
                    if r.mid:
                        pe.wait_ge(x1T_copied, r.m)
                    else:
                        if r.t1:
                            pe.wait_ge(sum3_done, r.t1)
                    for p in range(PAIRS):
                        h = p % HQ
                        mm = pe.matmul(tail_ps[STRIP * h:STRIP * (h + 1), 0, (p // HQ) * S:(p // HQ + 1) * S],
                                       vx_ones[:, p, :], probsx[:, p, :], start=True, stop=True,
                                       tile_position=(0, STRIP * h))
                    mm.then_inc(pvx_done, 1)
                if r.mid:
                    pe.wait_ge(ctxT_copied, r.m)
                    pe.matmul(prep_ps[:, 0:SC], c2("wkx"), ctxT2[:, 0:SC], start=True, stop=True)
                    pe.matmul(prep_ps[:, P:2 * P], ctxT2[:], c2("wvx"), start=True, stop=True).then_inc(kvx_made, 1)
                if r.self_:
                    exp_scores(2, 1, r.s, exp_done[2][0], r.s)
                if r.tail:
                    pe.wait_ge(pvx_copied, r.t)
                    if r.mid:
                        pe.wait_ge(qx_copied, r.m)
                    for t in range(QT):
                        for j in range(2):
                            mm = pe.transpose(tail_ps[:, 1, (2 * t + j) * P:(2 * t + j + 1) * P],
                                              attvT[:, j, t * P:(t + 1) * P], ident)
                    mm.then_inc(pvxT_made, 1)
                if r.self_:
                    if r.mid:
                        if r.m:
                            pe.wait_ge(kx_copied, r.m)
                        if r.m:
                            pe.wait_ge(vx_copied, r.m)
                    max_transposes(3, r.s)
                if r.tail:
                    pe.wait_ge(att2_done, r.t)
                    for t in range(QT):
                        mm = pe.transpose(tail_ps[:, 0, t * P:(t + 1) * P], att2[:, t, :], ident)
                    mm.then_inc(att2T_made, 1)
                if r.prep:
                    max_scores(0, 0, r.n, max_done[3][1], r.s)
                if r.self_:
                    exp_scores(3, 0, r.s, exp_done[2][1], r.s)
                if r.tail:
                    pe.wait_ge(att2T_copied, r.t)
                    for t in range(QT):
                        mm = pe.matmul(tail_ps[:, 1, t * P:(t + 1) * P], att2T[:, t * P:(t + 1) * P], c2("dense"),
                                       start=True, stop=True)
                    mm.then_inc(dense_made, 1)
                if r.prep:
                    max_scores(0, 1, r.n, max_done[0][0], r.n)
                if r.self_:
                    pv(2, r.s, r.m)
                    exp_scores(3, 1, r.s, exp_done[3][0], r.s)
                if r.tail:
                    pe.wait_ge(x2_done, r.t)
                    for t in range(QT):
                        mm = pe.transpose(tail_ps[:, 0, t * P:(t + 1) * P], x2[:, t, :], ident)
                    mm.then_inc(x2T_made, 1)
                if r.prep:
                    pe.wait_ge(v_copied, r.n)
                    max_transposes(0, r.n)
                if r.tail:
                    pe.wait_ge(x2T_copied, r.t)
                    for c in range(FC):
                        mm = pe.matmul(tail_ps[:, c // 2, (c % 2) * S:(c % 2 + 1) * S], c2("w1")[:, c * P:(c + 1) * P],
                                       x2T[:], start=True, stop=True)
                    mm.then_inc(h_made, 1)
                    pe.wait_ge(h_copied, r.t)
                    for t in range(QT):
                        for c in range(FC):
                            mm = pe.matmul(tail_ps[:, 0, t * P:(t + 1) * P], hT[:, c, t * P:(t + 1) * P],
                                           c2("w2")[:, c * D:(c + 1) * D], start=(c == 0), stop=(c == FC - 1))
                    mm.then_inc(ffn_made, 1)

            pe.wait_ge(consts_ready, 1)
            pe.wait_ge(later_in, 16)
            iterations(pe, "pe", body)

        @block.scalar
        def _(act):
            def exp(g, half, done, previous):
                act.wait_ge(exp_ready[g][half], done)
                if half == 0:
                    used = done if g >= 2 else previous
                    if used:
                        act.wait_ge(pv_done[(g + 2) % QUADS], used)
                nc.scalar.activation(probs[:, g % 2, 2 * half:2 * half + 2, :, :], scores_kq[:], ACT.Exp
                                     ).then_inc(exp_done[g][half], 1)

            def maxT(g, done):
                act.wait_ge(maxT_made[g], done)
                nc.scalar.copy(slots[NROWS:NROWS + MROWS, g, 0, :].bitcast(F32R), prep_ps[0:MROWS, 0:S]
                               ).then_inc(maxT_in[g], 1)

            def pv_copy(half, done, previous):
                act.wait_ge(pv_done[2 * half + 1], done)
                if previous:
                    act.wait_ge(pvT_made, previous)
                nc.scalar.copy(ctxvT[:, 2 * half:2 * half + 2, :], pv_acc[:]).then_inc(pv_copied[half], 1)

            def body(r):
                if r.self_:
                    exp(0, 0, r.s, r.m)
                if r.prep:
                    act.wait_ge(xT_made, r.n)
                    if r.s:
                        act.wait_ge(v_made, r.s)
                    nc.scalar.copy(xT[:], prep_ps[:, 0:S]).then_inc(xT_copied, 1)
                if r.mid:
                    pv_copy(1, r.m, r.t)
                if r.self_:
                    exp(0, 1, r.s, r.m)
                if r.prep:
                    act.wait_ge(qk_made, r.n)
                    if r.s:
                        act.wait_ge(rope_cos, r.s)
                    if r.s:
                        act.wait_ge(qk_swap_in, r.s_32)
                    nc.scalar.activation(qk[:, 0, :], prep_ps[:, 0:S], ACT.Identity, bias=c1("bq"))
                    nc.scalar.activation(qk[:, 1, :], prep_ps[:, S:2 * S], ACT.Identity, bias=c1("bk")).then_inc(qk_copied, 1)
                if r.self_:
                    maxT(1, r.s)
                if r.self_:
                    exp(1, 0, r.s, r.m)
                if r.tail:
                    act.wait_ge(maxxT_made, r.t)
                    for g in range(QUADS):
                        ins = nc.scalar.copy(qx_slots[NROWS:NROWS + MROWS, g, :].bitcast(F32R),
                                             prep_ps[STRIP * g:STRIP * g + MROWS, 0:S])
                    ins.then_inc(maxxT_in, 1)
                if r.mid:
                    act.wait_ge(x1T_made, r.m)
                    nc.scalar.copy(x1T[:], tail_ps[:, 0, 0:S]).then_inc(x1T_copied, 1)
                if r.self_:
                    exp(1, 1, r.s, r.m)
                    maxT(2, r.s)
                if r.tail:
                    act.wait_ge(expx_ready[0], r.t)
                    if r.t1:
                        act.wait_ge(pvx_done, r.t1)
                    nc.scalar.activation(probsx[:, 0:4, :], scores_kq[:], ACT.Exp).then_inc(expx_done[0], 1)
                if r.mid:
                    act.wait_ge(qx_made, r.m)
                    if r.t:
                        act.wait_ge(qx_lo_done, r.t)
                    nc.scalar.activation(qx[:], tail_ps[:, 1, 0:S], ACT.Identity, bias=c2("bqx")).then_inc(qx_copied, 1)
                if r.tail:
                    act.wait_ge(expx_ready[1], r.t)
                    nc.scalar.activation(probsx[:, 4:8, :], scores_kq[:], ACT.Exp).then_inc(expx_done[1], 1)
                if r.self_:
                    exp(2, 0, r.s, r.m)
                if r.mid:
                    act.wait_ge(ctxT_made, r.m)
                    if r.t:
                        act.wait_ge(kvx_made, r.t)
                    nc.scalar.copy(ctxT2[:], prep_ps[:, 0:P]).then_inc(ctxT_copied, 1)
                if r.self_:
                    pv_copy(0, r.s, r.m)
                if r.tail:
                    act.wait_ge(pvx_done, r.t)
                    if r.t1:
                        act.wait_ge(pvxT_made, r.t1)
                    nc.scalar.copy(attvT[:], tail_ps[:, 0, :]).then_inc(pvx_copied, 1)
                if r.self_:
                    exp(2, 1, r.s, r.m)
                    maxT(3, r.s)
                if r.tail:
                    act.wait_ge(att2T_made, r.t)
                    if r.t1:
                        act.wait_ge(dense_made, r.t1)
                    nc.scalar.copy(att2T[:], tail_ps[:, 0, 0:S]).then_inc(att2T_copied, 1)
                if r.self_:
                    exp(3, 0, r.s, r.m)
                    exp(3, 1, r.s, r.m)
                if r.tail:
                    act.wait_ge(x2T_made, r.t)
                    if r.t1:
                        act.wait_ge(h_made, r.t1)
                    nc.scalar.copy(x2T[:], tail_ps[:, 0, 0:S]).then_inc(x2T_copied, 1)
                if r.prep:
                    maxT(0, r.n)
                if r.tail:
                    act.wait_ge(h_made, r.t)
                    if r.t1:
                        act.wait_ge(ffn_made, r.t1)
                    for c in range(FC):
                        ins = nc.scalar.activation(hT[:, c, :], tail_ps[:, c // 2, (c % 2) * S:(c % 2 + 1) * S],
                                                   ACT.Relu, bias=c2("b1")[:, c:c + 1])
                    ins.then_inc(h_copied, 1)

            act.wait_ge(first_in, 16)
            act.wait_ge(later_in, 16)
            act.wait_ge(zeroed, 3)
            iterations(act, "act", body)

        @block.vector
        def _(dve):
            nc.vector.memset(slots[NROWS:P, :, 0, :], 0.0)
            nc.vector.memset(slots[NROWS:P, :, 1, :], 1.0)
            nc.vector.memset(qx_slots[NROWS:P, :, :], 0.0)
            nc.vector.memset(kx_slots[NROWS:P, :, :], 1.0)
            nc.vector.memset(minus_half[:], -0.5)
            nc.vector.memset(maxx_parts[:], 0.0).then_inc(zeroed, 1)
            nc.vector.memset(v_ones[:], 0.0).then_inc(zeroed, 1)
            nc.vector.memset(vx_ones[:], 0.0).then_inc(zeroed, 1)
            dve.wait_ge(zeroed, 3)
            nc.vector.memset(v_ones[:, :, :, HD:HD + 1], 1.0).then_inc(mask_step, 1)
            nc.vector.memset(vx_ones[0:SC, :, HD:HD + 1], 1.0)
            nc.vector.memset(vx_ones[SC:P, :, 16 + HD:16 + HD + 1], 1.0)
            dve.wait_ge(later_in, 16)
            nc.vector.tensor_copy(key_of_row[:].bitcast(F32R), c2("key_of_row"))
            nc.vector.tensor_scalar(mask_neg[:], c2("mask"), MASK_SCALE, None, ALU.mult).then_inc(mask_step, 1)
            dve.wait_ge(mask_step, 2)
            nc.vector.tensor_copy(mask_hi[:].bitcast(F32R), mask_neg[:])
            nc.vector.tensor_copy(mask_parts[0:SC, :].bitcast(F32R), mask_neg[0:SC, :]).then_inc(mask_step, 1)
            dve.wait_ge(mask_step, 3)
            nc.vector.tensor_tensor(mask_parts[SC:P, :].bitcast(F32R), mask_neg[SC:P, :], mask_hi[SC:P, :], ALU.subtract
                                    ).then_inc(consts_ready, 1)

            def reduce(g, t, done):
                dve.wait_ge(max_ready[g][t], done)
                nc.vector.tensor_reduce(neg_max[:, g, t, :], scores_qk[:].rearrange("p (h k) -> p h k", k=S), AX.X,
                                        ALU.max, negate=True).then_inc(max_done[g][t], 1)

            def split_max(g, done):
                dve.wait_ge(max_done[g][1], done)
                nc.vector.tensor_copy(max_parts[:, g, :, 0:HQ].bitcast(F32R), neg_max[:, g, :, :]).then_inc(max_hi_done[g], 1)
                dve.wait_ge(max_hi_done[g], done)
                nc.vector.tensor_tensor(max_parts[:, g, :, HQ:MROWS].bitcast(F32R), neg_max[:, g, :, :],
                                        max_parts[:, g, :, 0:HQ], ALU.subtract).then_inc(max_split[g], 1)

            def layer_norm(n, src, src_done, out, out_done, done):
                dve.wait_ge(src_done, done)
                for t in range(QT):
                    ins = nc.vector.bn_stats(stats[:, n, t, :], src[:, t, :])
                ins.then_inc(stats_done[n], 1)
                fixed_wait(dve)
                dve.wait_ge(stats_done[n], done)
                for t in range(QT):
                    ins = nc.vector.bn_aggr(mean_var[:, n, t, :], stats[:, n, t, :])
                ins.then_inc(aggr_done[n], 1)
                dve.wait_ge(aggr_done[n], done)
                nc.vector.tensor_scalar(var_eps[:, n, :], mean_var[:, n, :, 1], EPS, None, ALU.add).then_inc(var_done[n], 1)
                dve.wait_ge(rstd_done[n], done)
                for t in range(QT):
                    ins = nc.vector.tensor_scalar(out[:, t, :], src[:, t, :], mean_var[:, n, t, 0:1], rstd[:, n, t:t + 1],
                                                  ALU.subtract, ALU.mult)
                ins.then_inc(out_done, 1)

            def body(r):
                if r.self_:
                    reduce(1, 0, r.s)
                    reduce(1, 1, r.s)
                    split_max(1, r.s)
                if r.tail:
                    dve.wait_ge(maxx_ready[0], r.t)
                    nc.vector.tensor_reduce(neg_maxx[:, 0:QUADS, :], scores_qk[:].rearrange("p (h k) -> p h k", k=SC), AX.X,
                                            ALU.max, negate=True).then_inc(maxx_done[0], 1)
                    dve.wait_ge(maxx_ready[1], r.t)
                    nc.vector.tensor_reduce(neg_maxx[:, QUADS:2 * QUADS, :], scores_qk[:].rearrange("p (h k) -> p h k", k=SC),
                                            AX.X, ALU.max, negate=True).then_inc(maxx_done[1], 1)
                    dve.wait_ge(maxx_done[1], r.t)
                    if r.t1:
                        dve.wait_ge(maxxT_made, r.t1)
                    nc.vector.tensor_copy(maxx_parts[:, :, 0:HQ].bitcast(F32R), neg_maxx[:]).then_inc(maxx_hi_done, 1)
                    dve.wait_ge(maxx_hi_done, r.t)
                    nc.vector.tensor_tensor(maxx_parts[:, :, HQ:MROWS].bitcast(F32R), neg_maxx[:], maxx_parts[:, :, 0:HQ],
                                            ALU.subtract).then_inc(maxx_split, 1)
                if r.mid:
                    dve.wait_ge(pvT_made, r.m)
                    pvT = tail_ps[:].rearrange("p t (h c) -> p (t h) c", c=STRIP)
                    nc.vector.reciprocal(recip1[:], pvT[:, :, HD]).then_inc(recip1_done, 1)
                    dve.wait_ge(recip1_done, r.m)
                    nc.vector.tensor_tensor(att1[:].rearrange("p t (h c) -> p (t h) c", c=HD), pvT[:, :, 0:HD],
                                            recip1[:].rearrange("p (h o) -> p h o", o=1).to_broadcast([P, QT * H, HD]),
                                            ALU.mult).then_inc(att1_done, 1)
                    dve.wait_ge(att1_done, r.m)
                    dve.wait_ge(xres_loaded, r.m_16)
                    nc.vector.tensor_tensor(sum1[:], att1[:], x_res[:], ALU.add).then_inc(sum1_done, 1)
                    if r.t:
                        dve.wait_ge(x1b_done, r.t)
                    if r.t:
                        dve.wait_ge(x1T_made, r.t)
                    layer_norm(0, sum1, sum1_done, x1, x1_done, r.m)
                if r.self_:
                    reduce(2, 0, r.s)
                if r.prep:
                    dve.wait_ge(v_made, r.n)
                    if r.s:
                        dve.wait_ge(v_placed, r.s)
                    nc.vector.tensor_copy(v_rows[:], prep_ps[:, 0:S].rearrange("p (t d) -> p t d", t=QT)).then_inc(v_copied, 1)
                if r.self_:
                    reduce(2, 1, r.s)
                    split_max(2, r.s)
                if r.prep:
                    dve.wait_ge(rope_done, r.n)
                    for g in range(QUADS):
                        if r.s:
                            dve.wait_ge(slots_in[g], r.s_48)
                    nc.vector.tensor_copy(qk_parts[:, 0:4:2, :].bitcast(F32R), qk_rope[:]).then_inc(qk_hi_done, 1)
                if r.mid:
                    dve.wait_ge(qx_copied, r.m)
                    if r.t:
                        dve.wait_ge(qx_out, r.t_16)
                    nc.vector.tensor_copy(qx_parts[:, 0, :].bitcast(F32R), qx[:]).then_inc(qx_hi_done, 1)
                if r.self_:
                    reduce(3, 0, r.s)
                    reduce(3, 1, r.s)
                if r.mid:
                    dve.wait_ge(kvx_made, r.m)
                    if r.t:
                        dve.wait_ge(kx_lo_done, r.t)
                    nc.vector.tensor_scalar(kx[:], prep_ps[:, 0:SC], c2("bkx"), KSCALE, ALU.add, ALU.mult).then_inc(kx_copied, 1)
                    if r.t:
                        dve.wait_ge(pvx_done, r.t)
                    for j in range(2):
                        rows = slice(j * SC, (j + 1) * SC)
                        ins = nc.vector.tensor_tensor(
                            vx_ones[rows, :, 16 * j:16 * j + HD],
                            prep_ps[rows, P:2 * P].rearrange("p (a j c) -> p a j c", j=2, c=HD)[:, :, j, :],
                            c2("bvx")[rows, :].rearrange("p (a j c) -> p a j c", j=2, c=HD)[:, :, j, :], ALU.add)
                    ins.then_inc(vx_copied, 1)
                    dve.wait_ge(kx_copied, r.m)
                    if r.t:
                        dve.wait_ge(kx_out, r.t_16)
                    nc.vector.tensor_copy(kx_parts[:, 0, :].bitcast(F32R), kx[:]).then_inc(kx_hi_done, 1)
                    dve.wait_ge(kx_hi_done, r.m)
                    nc.vector.tensor_tensor(kx_parts[:, 1, :].bitcast(F32R), kx[:], kx_parts[:, 0, :], ALU.subtract
                                            ).then_inc(kx_lo_done, 1)
                if r.self_:
                    split_max(3, r.s)
                if r.tail:
                    dve.wait_ge(pvxT_made, r.t)
                    pvxT = tail_ps[:, 1, :].rearrange("p (h c) -> p h c", c=16)
                    nc.vector.reciprocal(recip2[:], pvxT[:, :, HD]).then_inc(recip2_done, 1)
                    dve.wait_ge(recip2_done, r.t)
                    nc.vector.tensor_tensor(att2[:].rearrange("p t (h c) -> p (t h) c", c=HD), pvxT[:, :, 0:HD],
                                            recip2[:].rearrange("p (h o) -> p h o", o=1).to_broadcast([P, QT * H, HD]),
                                            ALU.mult).then_inc(att2_done, 1)
                if r.prep:
                    reduce(0, 0, r.n)
                if r.tail:
                    dve.wait_ge(dense_made, r.t)
                    dve.wait_ge(x1b_done, r.t)
                    nc.vector.tensor_tensor(sum2[:], tail_ps[:, 1, 0:S].rearrange("p (t d) -> p t d", t=QT), x1_bias[:],
                                            ALU.add).then_inc(sum2_done, 1)
                if r.prep:
                    reduce(0, 1, r.n)
                    split_max(0, r.n)
                if r.tail:
                    layer_norm(1, sum2, sum2_done, x2, x2_done, r.t)
                    dve.wait_ge(ffn_made, r.t)
                    dve.wait_ge(x2b_done, r.t)
                    nc.vector.tensor_tensor(sum3[:], tail_ps[:, 0, 0:S].rearrange("p (t d) -> p t d", t=QT), x2_bias[:],
                                            ALU.add).then_inc(sum3_done, 1)
                    if r.t1:
                        dve.wait_ge(stored, r.t1_16)
                    layer_norm(2, sum3, sum3_done, y, y_done, r.t)

            dve.wait_ge(first_in, 16)
            iterations(dve, "dve", body)

        @block.gpsimd
        def _(pool):
            def inverse_std(n, done):
                pool.wait_ge(var_done[n], done)
                nc.gpsimd.tensor_tensor(rstd[:, n, :], var_eps[:, n, :], minus_half[:], ALU.pow).then_inc(rstd_done[n], 1)

            row_head = c1("head_of_row").rearrange("p (h o) -> p h o", o=1)

            def diagonal(g, loaded, used):
                pool.wait_ge(slots_in[g], loaded)
                if used:
                    pool.wait_ge(exp_ready[g][1], used)
                nc.gpsimd.tensor_tensor(k_diag[:, g, :, :].bitcast(F32R),
                                        slots[:, g, 1:2, :].to_broadcast([P, HQ, S]),
                                        row_head.to_broadcast([P, HQ, S]), ALU.mult).then_inc(diag_done[g], 1)

            def body(r):
                if r.self_:
                    diagonal(3, r.s_48, r.m)
                    pool.wait_ge(v_copied, r.s)
                    if r.m:
                        pool.wait_ge(pv_done[3], r.m)
                    for t in range(QT):
                        ins = nc.gpsimd.tensor_tensor(v_ones[:, t, :, 0:HD], v_rows[:, t, :].rearrange("p (h c) -> p h c", c=HD),
                                                      c1("bv").rearrange("p (h c) -> p h c", c=HD), ALU.add)
                    ins.then_inc(v_placed, 1)
                if r.prep:
                    pool.wait_ge(qk_copied, r.n)
                    if r.s:
                        pool.wait_ge(rope_done, r.s)
                    nc.gpsimd.tensor_tensor(qk_cos[:], qk[:], c1("cos").rearrange("p (j c) -> p j c", j=2), ALU.mult
                                            ).then_inc(rope_cos, 1)
                    pool.wait_ge(qk_swap_in, r.n_32)
                    nc.gpsimd.tensor_tensor(qk_sin[:], qk_swapped[:], c1("sin").rearrange("p (j c) -> p j c", j=2), ALU.mult
                                            ).then_inc(rope_sin, 1)
                    pool.wait_ge(rope_cos, r.n)
                    pool.wait_ge(rope_sin, r.n)
                    if r.s:
                        pool.wait_ge(qk_lo_done, r.s)
                    nc.gpsimd.tensor_tensor(qk_rope[:], qk_cos[:], qk_sin[:], ALU.add).then_inc(rope_done, 1)
                if r.mid:
                    inverse_std(0, r.m)
                if r.prep:
                    pool.wait_ge(qk_hi_done, r.n)
                    nc.gpsimd.tensor_tensor(qk_parts[:, 1:4:2, :].bitcast(F32R), qk_rope[:], qk_parts[:, 0:4:2, :],
                                            ALU.subtract).then_inc(qk_lo_done, 1)
                if r.mid:
                    pool.wait_ge(qx_hi_done, r.m)
                    nc.gpsimd.tensor_tensor(qx_parts[:, 1, :].bitcast(F32R), qx[:], qx_parts[:, 0, :], ALU.subtract
                                            ).then_inc(qx_lo_done, 1)
                if r.prep:
                    diagonal(0, r.n_48, r.s)
                    diagonal(1, r.n_48, r.s)
                    diagonal(2, r.n_48, r.s)
                if r.mid:
                    pool.wait_ge(kx_slots_in, r.m_48)
                    if r.t:
                        pool.wait_ge(expx_ready[1], r.t)
                    for g in range(QUADS):
                        ins = nc.gpsimd.tensor_tensor(kx_diag[:, g, :, :].bitcast(F32R),
                                                      kx_slots[:, g:g + 1, :].to_broadcast([P, HQ, SC]),
                                                      row_head.to_broadcast([P, HQ, SC]), ALU.mult)
                    ins.then_inc(kx_diag_done, 1)
                if r.tail:
                    inverse_std(1, r.t)
                    pool.wait_ge(x2_done, r.t)
                    if r.t1:
                        pool.wait_ge(sum3_done, r.t1)
                    nc.gpsimd.tensor_tensor(x2_bias[:], x2[:], c2("b2").rearrange("p (o d) -> p o d", o=1)
                                            .to_broadcast([P, QT, D]), ALU.add).then_inc(x2b_done, 1)
                if r.mid:
                    pool.wait_ge(x1_done, r.m)
                    if r.t:
                        pool.wait_ge(sum2_done, r.t)
                    nc.gpsimd.tensor_tensor(x1_bias[:], x1[:], c2("dense_b").rearrange("p (o d) -> p o d", o=1)
                                            .to_broadcast([P, QT, D]), ALU.add).then_inc(x1b_done, 1)
                if r.tail:
                    inverse_std(2, r.t)

            pool.wait_ge(first_in, 16)
            pool.wait_ge(later_in, 16)
            pool.wait_ge(zeroed, 3)
            pool.wait_ge(consts_ready, 1)
            iterations(pool, "pool", body)


def shape_constants():
    import numpy as np

    row = np.arange(P)
    dim = row % HD
    inv = np.power(np.float32(10000.0), -2.0 * np.arange(HD // 2, dtype=np.float32) / np.float32(HD)).astype(np.float32)
    angle = (np.arange(S, dtype=np.float32)[None, :] * inv[dim // 2][:, None]).astype(np.float32)
    sign = np.where(dim % 2 == 0, -1.0, 1.0)[:, None]
    scale = np.array([1.0, KSCALE])[None, :, None]
    cos = (np.cos(angle.astype(np.float64))[:, None, :] * scale).reshape(P, 2 * S)
    sin = ((sign * np.sin(angle.astype(np.float64)))[:, None, :] * scale).reshape(P, 2 * S)
    head = np.where(row < NROWS, (row % QROWS) // HD, np.where(row < NROWS + MROWS, row % HQ, -1))
    return {
        "ident": np.eye(P, dtype=np.float32),
        "cos": cos.astype(np.float32),
        "sin": sin.astype(np.float32),
        "head_of_row": (head[:, None] == np.arange(HQ)[None, :]).astype(np.float32),
        "key_of_row": (row[:, None] % SC == np.arange(8 * SC)[None, :] % SC).astype(np.float32),
    }


def kernel(**inputs):
    import numpy as np
    import concourse.bacc as bacc
    from concourse.bass_utils import run_bass_kernel_spmd

    a = {k: np.asarray(v) for k, v in inputs.items()}
    column = lambda v: v.reshape(-1, P).T
    every_row = lambda v: np.broadcast_to(v[None, :], (P, v.shape[0]))
    maskT = a["mask_1x1xSxS2_fk1"][0, 0].T
    parts = dict(shape_constants())
    parts.update(
        wq=a["L0_attn_Wq"], wk=a["L0_attn_Wk"], wv=a["L0_attn_Wv"],
        bq=column(a["L0_attn_bq"]), bk=column(a["L0_attn_bk"]), bv=every_row(a["L0_attn_bv"]),
        wqx=a["L0_xattn_wq_w"].T, wkx=a["L0_xattn_wk_w"].T, wvx=a["L0_xattn_wv_w"].T, dense=a["L0_xattn_dense_w"].T,
        w1=a["L0_ffn_W1"], w2=a["L0_ffn_W2"].reshape(FC, P, D).transpose(1, 0, 2).reshape(P, FC * D),
        bqx=column(a["L0_xattn_wq_b"]), bkx=column(a["L0_xattn_wk_b"]), b1=column(a["L0_ffn_b1"]),
        bvx=every_row(a["L0_xattn_wv_b"]), dense_b=every_row(a["L0_xattn_dense_b"]), b2=every_row(a["L0_ffn_b2"]),
        mask=np.concatenate([maskT, maskT], axis=0),
    )
    arrays = {
        "x": np.ascontiguousarray(a["x"]),
        "ctx": np.ascontiguousarray(a["ctx_1024"]),
        "first": np.ascontiguousarray(np.concatenate([parts[n] for n, _ in FIRST], axis=1)),
        "later": np.ascontiguousarray(np.concatenate([parts[n] for n, _ in LATER], axis=1)),
    }
    nc = bacc.Bacc("TRN2", target_bir_lowering=False, num_devices=1)
    args = [nc.dram_tensor(n, v.shape, mybir.dt.from_np(v.dtype), kind="ExternalInput").ap() for n, v in arrays.items()]
    out = nc.dram_tensor("out", (B, S, D), F32, kind="ExternalOutput").ap()
    build(nc, *args, out)
    return run_bass_kernel_spmd(nc, [arrays], core_ids=[0]).results[0]["out"]
```

```python
from contextlib import ExitStack

import concourse.bass as bass
from concourse import mybir

F32 = mybir.dt.float32
F32R = mybir.dt.float32r
ALU = mybir.AluOpType
ACT = mybir.ActivationFunctionType
AX = mybir.AxisListType

P = 128
B, S, D = 8, 256, 128
SC = 64
H, HD = 16, 8
FF = 512
QT = S // P
QUADS, HQ = 4, 4
PAIRS = H // 2
FC = FF // P
STRIP = 32
QROWS = HQ * HD
NROWS = 3 * QROWS
MROWS = 2 * HQ
EPS = 1e-5
MASK_SCALE = -1e9
KSCALE = HD ** -0.5

FIRST = [("ident", P), ("wq", D), ("wk", D), ("wv", D), ("bq", 1), ("bk", 1), ("cos", 2 * S), ("sin", 2 * S),
         ("head_of_row", HQ), ("bv", D)]
LATER = [("wqx", D), ("wkx", D), ("wvx", D), ("dense", D), ("w1", FF), ("w2", FC * D), ("bqx", 1), ("bkx", 1),
         ("b1", FC), ("bvx", D), ("dense_b", D), ("b2", D), ("mask", S), ("key_of_row", 8 * SC)]


def columns(fields):
    at, n = {}, 0
    for name, width in fields:
        at[name] = (n, width)
        n += width
    return at, n


FIRST_AT, FIRST_N = columns(FIRST)
LATER_AT, LATER_N = columns(LATER)


def build(nc, x_d, ctx_d, first_d, later_d, out_d):
    with ExitStack() as ctx:
        def sb(name, shape):
            return ctx.enter_context(nc.sbuf_tensor(name, shape, F32))

        def psum(name, shape):
            return ctx.enter_context(nc.psum_tensor(name, shape, F32))

        def sem(name):
            return ctx.enter_context(nc.semaphore(name))

        def sems(name, n):
            return [sem(f"{name}{j}") for j in range(n)]

        qx_scratch = nc.dram_tensor("qx_scratch", [P, 2, S], F32, kind="Internal").ap()
        kx_scratch = nc.dram_tensor("kx_scratch", [P, 2, SC], F32, kind="Internal").ap()

        first = sb("first_sb", [P, FIRST_N])
        later = sb("later_sb", [P, LATER_N])

        def c1(name):
            a, w = FIRST_AT[name]
            return first[:, a:a + w]

        def c2(name):
            a, w = LATER_AT[name]
            return later[:, a:a + w]

        x_in = sb("x_in", [P, QT, D])
        x_res = sb("x_res", [P, QT, D])
        ctx_in = sb("ctx_in", [P, D])
        xT = sb("xT", [P, S])
        qk = sb("qk", [P, 2, S])
        qk_swapped = sb("qk_swapped", [P, 2, S])
        qk_cos = sb("qk_cos", [P, 2, S])
        qk_sin = sb("qk_sin", [P, 2, S])
        qk_rope = sb("qk_rope", [P, 2, S])
        qk_parts = sb("qk_parts", [P, 4, S])
        slots = sb("slots", [P, QUADS, 2, S])
        k_diag = sb("k_diag", [P, QUADS, HQ, S])
        v_rows = sb("v_rows", [P, QT, D])
        v_ones = sb("v_ones", [P, QT, H, STRIP])
        neg_max = sb("neg_max", [P, QUADS, QT, HQ])
        max_parts = sb("max_parts", [P, QUADS, QT, MROWS])
        probs = sb("probs", [P, 2, HQ, QT, S])
        ctxvT = sb("ctxvT", [P, QUADS, S])
        recip1 = sb("recip1", [P, QT * H])
        att1 = sb("att1", [P, QT, D])
        sum1 = sb("sum1", [P, QT, D])
        x1 = sb("x1", [P, QT, D])
        x1_bias = sb("x1_bias", [P, QT, D])
        x1T = sb("x1T", [P, S])
        qx = sb("qx", [P, S])
        qx_parts = sb("qx_parts", [P, 2, S])
        qx_slots = sb("qx_slots", [P, QUADS, S])
        ctxT2 = sb("ctxT2", [P, 2 * SC])
        kx = sb("kx", [P, SC])
        kx_parts = sb("kx_parts", [P, 2, SC])
        kx_slots = sb("kx_slots", [P, QUADS, SC])
        kx_diag = sb("kx_diag", [P, QUADS, HQ, SC])
        vx_ones = sb("vx_ones", [P, PAIRS, STRIP])
        neg_maxx = sb("neg_maxx", [P, QT * QUADS, HQ])
        maxx_parts = sb("maxx_parts", [P, QT * QUADS, STRIP])
        probsx = sb("probsx", [P, PAIRS, S])
        attvT = sb("attvT", [P, 2, S])
        recip2 = sb("recip2", [P, QT * H])
        att2 = sb("att2", [P, QT, D])
        att2T = sb("att2T", [P, S])
        sum2 = sb("sum2", [P, QT, D])
        x2 = sb("x2", [P, QT, D])
        x2_bias = sb("x2_bias", [P, QT, D])
        x2T = sb("x2T", [P, S])
        hT = sb("hT", [P, FC, S])
        sum3 = sb("sum3", [P, QT, D])
        y = sb("y", [P, QT, D])
        stats = sb("stats", [P, 3, QT, 6])
        mean_var = sb("mean_var", [P, 3, QT, 2])
        var_eps = sb("var_eps", [P, 3, QT])
        rstd = sb("rstd", [P, 3, QT])
        minus_half = sb("minus_half", [P, QT])
        mask_neg = sb("mask_neg", [P, S])
        mask_parts = sb("mask_parts", [P, S])
        mask_hi = sb("mask_hi", [P, S])
        key_of_row = sb("key_of_row", [P, 8 * SC])

        scores_qk = psum("scores_qk", [P, 1024])
        scores_kq = psum("scores_kq", [P, 1024])
        pv_acc = psum("pv_acc", [P, 2, S])
        prep_ps = psum("prep_ps", [P, 512])
        tail_ps = psum("tail_ps", [P, 2, 512])

        first_in, later_in, zeroed, consts_ready = sem("first_in"), sem("later_in"), sem("zeroed"), sem("consts_ready")
        mask_step = sem("mask_step")
        x_loaded, xres_loaded, ctx_loaded = sem("x_loaded"), sem("xres_loaded"), sem("ctx_loaded")
        xT_made, xT_copied = sem("xT_made"), sem("xT_copied")
        qk_made, qk_copied, qk_swap_in = sem("qk_made"), sem("qk_copied"), sem("qk_swap_in")
        rope_cos, rope_sin, rope_done = sem("rope_cos"), sem("rope_sin"), sem("rope_done")
        qk_hi_done, qk_lo_done = sem("qk_hi_done"), sem("qk_lo_done")
        v_made, v_copied, v_placed = sem("v_made"), sem("v_copied"), sem("v_placed")
        slots_in, diag_done = sems("slots_in", QUADS), sems("diag_done", QUADS)
        max_ready = [sems(f"max_ready{g}_", QT) for g in range(QUADS)]
        max_done = [sems(f"max_done{g}_", QT) for g in range(QUADS)]
        max_hi_done, max_split = sems("max_hi_done", QUADS), sems("max_split", QUADS)
        maxT_made, maxT_in = sems("maxT_made", QUADS), sems("maxT_in", QUADS)
        exp_ready = [sems(f"exp_ready{g}_", 2) for g in range(QUADS)]
        exp_done = [sems(f"exp_done{g}_", 2) for g in range(QUADS)]
        pv_done = sems("pv_done", QUADS)
        pv_copied = sems("pv_copied", 2)
        pvT_made = sem("pvT_made")
        recip1_done, att1_done, sum1_done = sem("recip1_done"), sem("att1_done"), sem("sum1_done")
        stats_done, aggr_done, var_done, rstd_done = (sems(n, 3) for n in ("stats_done", "aggr_done", "var_done", "rstd_done"))
        x1_done, x1b_done, x1T_made, x1T_copied = sem("x1_done"), sem("x1b_done"), sem("x1T_made"), sem("x1T_copied")
        qx_made, qx_copied, qx_hi_done, qx_lo_done = sem("qx_made"), sem("qx_copied"), sem("qx_hi_done"), sem("qx_lo_done")
        qx_out, qx_slots_in = sem("qx_out"), sem("qx_slots_in")
        ctxT_made, ctxT_copied = sem("ctxT_made"), sem("ctxT_copied")
        kvx_made, kx_copied, vx_copied = sem("kvx_made"), sem("kx_copied"), sem("vx_copied")
        kx_hi_done, kx_lo_done, kx_out, kx_slots_in = sem("kx_hi_done"), sem("kx_lo_done"), sem("kx_out"), sem("kx_slots_in")
        kx_diag_done = sem("kx_diag_done")
        maxx_ready, maxx_done = sems("maxx_ready", QT), sems("maxx_done", QT)
        maxx_hi_done, maxx_split, maxxT_made, maxxT_in = sem("maxx_hi_done"), sem("maxx_split"), sem("maxxT_made"), sem("maxxT_in")
        expx_ready, expx_done = sems("expx_ready", 2), sems("expx_done", 2)
        pvx_done, pvx_copied, pvxT_made = sem("pvx_done"), sem("pvx_copied"), sem("pvxT_made")
        recip2_done, att2_done, att2T_made, att2T_copied = sem("recip2_done"), sem("att2_done"), sem("att2T_made"), sem("att2T_copied")
        dense_made, sum2_done, x2_done, x2b_done = sem("dense_made"), sem("sum2_done"), sem("x2_done"), sem("x2b_done")
        x2T_made, x2T_copied, h_made, h_copied = sem("x2T_made"), sem("x2T_copied"), sem("h_made"), sem("h_copied")
        ffn_made, sum3_done, y_done, stored = sem("ffn_made"), sem("sum3_done"), sem("y_done"), sem("stored")

        def fixed_wait(eng):
            eng.wait_ge(first_in, 16)

        FIRST_LOOPED, END_LOOPED = 3, B - 2

        class Counts:

            def __init__(self, at):
                self.w, self.n, self.s = at("w", 3, 1), at("n", 2, 1), at("s", 1, 1)
                self.m, self.t, self.u = at("m", 0, 1), at("t", -1, 1), at("u", -2, 1)

            def dma(self, at):
                self.w_16, self.w_32, self.n_32 = at("w16", 3, 16), at("w32", 3, 32), at("n32", 2, 32)
                self.n_48, self.s_48 = at("n48", 2, 48), at("s48", 1, 48)
                self.m_16, self.m_32, self.m_48 = at("m16", 0, 16), at("m32", 0, 32), at("m48", 0, 48)
                self.t_16, self.t_48, self.u_16 = at("t16", -1, 16), at("t48", -1, 48), at("u16", -2, 16)
                return self

        def peeled(e):
            number = lambda name, k, unit: min(max(0, e + k), B) * unit
            r = Counts(number).dma(number)
            r.e = e
            r.early, r.prep, r.self_ = e + 2 < B, 0 <= e + 1 < B, 0 <= e < B
            r.mid, r.tail, r.last = 0 <= e - 1 < B, 0 <= e - 2 < B, 0 <= e - 3 < B
            return r

        def iterations(eng, name, body):
            for e in range(-2, FIRST_LOOPED):
                body(peeled(e))
            registers = []

            def register(role, k, unit):
                reg = eng.alloc_register(f"{name}_{role}_runs")
                eng.reg_mov(reg, (FIRST_LOOPED + k) * unit)
                registers.append((reg, unit))
                return reg

            r = Counts(register).dma(register)
            r.early = r.prep = r.self_ = r.mid = r.tail = r.last = True
            with eng.Fori(FIRST_LOOPED, END_LOOPED) as e:
                r.e = e
                body(r)
                for reg, unit in registers:
                    eng.reg_add(reg, reg, unit)
            for e in range(END_LOOPED, B + 3):
                body(peeled(e))

        block = ctx.enter_context(nc.Block())

        @block.sync
        def _(sp):
            sp.dma_start(first[:], first_d).then_inc(first_in, 16)
            sp.dma_start(later[:], later_d).then_inc(later_in, 16)

            def slot_loads(g, made, used):
                sp.wait_ge(qk_lo_done, made)
                if used:
                    sp.wait_ge(exp_ready[g][1], used)
                if used:
                    sp.wait_ge(diag_done[g], used)
                for s, (qp, kp) in enumerate(((0, 2), (0, 3), (1, 2))):
                    sp.dma_start(slots[QROWS * s:QROWS * (s + 1), g, :, :],
                                 qk_parts[QROWS * g:QROWS * (g + 1), qp:kp + 1:kp - qp, :]).then_inc(slots_in[g], 16)

            def body(r):
                if r.early:
                    fixed_wait(sp)
                    if r.n:
                        sp.wait_ge(xT_made, r.n)
                    sp.dma_start(x_in[:], x_d[r.e + 2].rearrange("(t p) d -> p t d", p=P)).then_inc(x_loaded, 16)
                if r.self_:
                    slot_loads(3, r.s, r.m)
                if r.mid:
                    fixed_wait(sp)
                    if r.t:
                        sp.wait_ge(sum1_done, r.t)
                    sp.dma_start(x_res[:], x_d[r.e - 1].rearrange("(t p) d -> p t d", p=P)).then_inc(xres_loaded, 16)
                    fixed_wait(sp)
                    if r.t:
                        sp.wait_ge(ctxT_made, r.t)
                    for j in range(2):
                        sp.dma_start(ctx_in[j * SC:(j + 1) * SC, :], ctx_d[r.e - 1]).then_inc(ctx_loaded, 16)
                if r.prep:
                    slot_loads(0, r.n, r.s)
                    slot_loads(1, r.n, r.s)
                if r.mid:
                    sp.wait_ge(qx_lo_done, r.m)
                    if r.t:
                        sp.wait_ge(qx_slots_in, r.t_48)
                    sp.dma_start(qx_scratch, qx_parts[:]).then_inc(qx_out, 16)
                if r.early:
                    sp.wait_ge(qk_copied, r.w)
                    if r.n:
                        sp.wait_ge(rope_sin, r.n)
                    for half in range(2):
                        sp.dma_start(qk_swapped[half:P:2, :, :], qk[1 - half:P:2, :, :]).then_inc(qk_swap_in, 16)
                if r.mid:
                    sp.wait_ge(qx_out, r.m_16)
                    if r.t:
                        sp.wait_ge(expx_ready[1], r.t)
                    for s, part in enumerate((0, 0, 1)):
                        sp.dma_start(qx_slots[QROWS * s:QROWS * (s + 1), :, :],
                                     qx_scratch[:, part, :].rearrange("(g r) c -> r g c", g=QUADS)).then_inc(qx_slots_in, 16)
                    sp.wait_ge(kx_lo_done, r.m)
                    if r.t:
                        sp.wait_ge(kx_slots_in, r.t_48)
                    sp.dma_start(kx_scratch, kx_parts[:]).then_inc(kx_out, 16)
                if r.prep:
                    slot_loads(2, r.n, r.s)
                if r.mid:
                    sp.wait_ge(kx_out, r.m_16)
                    if r.t:
                        sp.wait_ge(kx_diag_done, r.t)
                    for s, part in enumerate((0, 1, 0)):
                        sp.dma_start(kx_slots[QROWS * s:QROWS * (s + 1), :, :],
                                     kx_scratch[:, part, :].rearrange("(g r) c -> r g c", g=QUADS)).then_inc(kx_slots_in, 16)
                if r.last:
                    fixed_wait(sp)
                    sp.wait_ge(y_done, r.u)
                    sp.dma_start(out_d[r.e - 3].rearrange("(t p) d -> p t d", p=P), y[:]).then_inc(stored, 16)

            iterations(sp, "sp", body)
            sp.wait_ge(stored, 16 * (B + 1))

        @block.tensor
        def _(pe):
            ident = c1("ident")
            sp_r, kd_r = slots[:].bitcast(F32R), k_diag[:].bitcast(F32R)
            qxs_r, kxd_r = qx_slots[:].bitcast(F32R), kx_diag[:].bitcast(F32R)
            mask_r, keys_r = mask_parts[:].bitcast(F32R), key_of_row[:].bitcast(F32R)

            def max_scores(g, t, done, free, free_count):
                pe.wait_ge(diag_done[g], done)
                if free_count:
                    pe.wait_ge(free, free_count)
                for h in range(0, HQ, 2):
                    mm = pe.matmul(scores_qk[:, h * S:(h + 2) * S], sp_r[0:NROWS, g, 0, t * P:(t + 1) * P],
                                   kd_r[0:NROWS, g, h:h + 2, :], start=True, stop=True)
                mm.then_inc(max_ready[g][t], 1)

            def exp_scores(g, half, done, free, free_count):
                if half == 0:
                    pe.wait_ge(maxT_in[g], done)
                if free_count:
                    pe.wait_ge(free, free_count)
                for j in range(2):
                    for kt in range(QT):
                        mm = pe.matmul(scores_kq[:, (2 * j + kt) * S:(2 * j + kt + 1) * S],
                                       kd_r[:, g, 2 * half + j, kt * P:(kt + 1) * P], sp_r[:, g, 0, :],
                                       start=True, stop=True)
                mm.then_inc(exp_ready[g][half], 1)

            def max_transposes(g, done):
                pe.wait_ge(max_split[g], done)
                for t in range(QT):
                    mm = pe.transpose(prep_ps[0:MROWS, t * P:(t + 1) * P], max_parts[:, g, t, :], ident)
                mm.then_inc(maxT_made[g], 1)

            def pv(g, done, previous):
                pe.wait_ge(exp_done[g][0], done)
                pe.wait_ge(exp_done[g][1], done)
                if g == 0:
                    pe.wait_ge(v_placed, done)
                    if previous:
                        pe.wait_ge(pv_copied[1], previous)
                if g == 2:
                    pe.wait_ge(pv_copied[0], done)
                for kt in range(QT):
                    for h in range(HQ):
                        mm = pe.matmul(pv_acc[STRIP * h:STRIP * (h + 1), g % 2, :], v_ones[:, kt, HQ * g + h, :],
                                       probs[:, g % 2, h, kt, :], start=(kt == 0), stop=(kt == QT - 1),
                                       tile_position=(0, STRIP * h))
                mm.then_inc(pv_done[g], 1)

            def maxx_scores(t, r):
                if t == 0:
                    if r.t:
                        pe.wait_ge(kx_diag_done, r.t)
                    if r.t:
                        pe.wait_ge(qx_slots_in, r.t_48)
                    if r.self_:
                        pe.wait_ge(max_done[1][1], r.s)
                    else:
                        pe.wait_ge(max_done[3][1], B)
                        pe.wait_ge(maxx_done[1], r.u)
                else:
                    if r.t:
                        pe.wait_ge(maxx_done[0], r.t)
                for half in range(2):
                    pe.matmul(scores_qk[:, half * 512:(half + 1) * 512], mask_r[:, t * P:(t + 1) * P], keys_r,
                              start=True, stop=False, skip_group_check=True)
                    for g in range(2 * half, 2 * half + 2):
                        mm = pe.matmul(scores_qk[:, g * 256:(g + 1) * 256], qxs_r[0:NROWS, g, t * P:(t + 1) * P],
                                       kxd_r[0:NROWS, g, :, :], start=False, stop=True, skip_group_check=True)
                mm.then_inc(maxx_ready[t], 1)

            def expx_scores(u, r):
                if u == 0:
                    if r.t:
                        pe.wait_ge(maxxT_in, r.t)
                    if r.self_:
                        pe.wait_ge(exp_done[1][1], r.s)
                    else:
                        pe.wait_ge(exp_done[3][1], B)
                        pe.wait_ge(expx_done[1], r.u)
                else:
                    if r.t:
                        pe.wait_ge(expx_done[0], r.t)
                for p in range(4 * u, 4 * u + 4):
                    o = scores_kq[:, (p % 4) * S:(p % 4 + 1) * S]
                    pe.matmul(o, keys_r[:, 0:P], mask_r, start=True, stop=False)
                    mm = pe.matmul(o, kxd_r[:, p // 2, 2 * (p % 2):2 * (p % 2) + 2, :], qxs_r[:, p // 2, :],
                                   start=False, stop=True)
                mm.then_inc(expx_ready[u], 1)

            def body(r):
                if r.self_:
                    max_scores(1, 0, r.s, max_done[0][1], r.s)
                    exp_scores(0, 0, r.s, exp_done[3][1], r.m)
                if r.mid:
                    pv(3, r.m, r.t)
                if r.self_:
                    max_scores(1, 1, r.s, max_done[1][0], r.s)
                    exp_scores(0, 1, r.s, exp_done[0][0], r.s)
                if r.prep:
                    if r.self_:
                        pe.wait_ge(maxT_in[0], r.s)
                    else:
                        pe.wait_ge(qk_copied, r.n)
                    for t in range(QT):
                        mm = pe.matmul(prep_ps[:, t * P:(t + 1) * P], xT[:, t * P:(t + 1) * P], c1("wv"),
                                       start=True, stop=True)
                    mm.then_inc(v_made, 1)
                if r.mid:
                    pe.wait_ge(pv_copied[1], r.m)
                    if r.u:
                        pe.wait_ge(sum2_done, r.u)
                    for t in range(QT):
                        for g in range(QUADS):
                            mm = pe.transpose(tail_ps[:, t, g * P:(g + 1) * P], ctxvT[:, g, t * P:(t + 1) * P], ident)
                    mm.then_inc(pvT_made, 1)
                if r.tail:
                    maxx_scores(0, r)
                if r.self_:
                    if r.prep:
                        pe.wait_ge(v_copied, r.n)
                    max_transposes(1, r.s)
                if r.last:
                    pe.wait_ge(x2_done, r.u)
                    if r.mid:
                        pe.wait_ge(att1_done, r.m)
                    for t in range(QT):
                        mm = pe.transpose(tail_ps[:, 0, t * P:(t + 1) * P], x2[:, t, :], ident)
                    mm.then_inc(x2T_made, 1)
                if r.tail:
                    maxx_scores(1, r)
                if r.self_:
                    exp_scores(1, 0, r.s, exp_done[0][1], r.s)
                    if r.tail:
                        pe.wait_ge(maxx_done[1], r.t)
                    max_scores(2, 0, r.s, max_done[1][1], r.s)
                if r.last:
                    pe.wait_ge(x2T_copied, r.u)
                    for c in range(FC):
                        mm = pe.matmul(tail_ps[:, c // 2, (c % 2) * S:(c % 2 + 1) * S], c2("w1")[:, c * P:(c + 1) * P],
                                       x2T[:], start=True, stop=True)
                    mm.then_inc(h_made, 1)
                if r.self_:
                    exp_scores(1, 1, r.s, exp_done[1][0], r.s)
                    max_scores(2, 1, r.s, max_done[2][0], r.s)
                    pv(0, r.s, r.m)
                if r.early:
                    pe.wait_ge(x_loaded, r.w_16)
                    if r.self_:
                        pe.wait_ge(maxT_in[1], r.s)
                    elif r.prep:
                        pe.wait_ge(v_copied, r.n)
                    for t in range(QT):
                        mm = pe.transpose(prep_ps[:, t * P:(t + 1) * P], x_in[:, t, :], ident)
                    mm.then_inc(xT_made, 1)
                if r.last:
                    pe.wait_ge(h_copied, r.u)
                    for t in range(QT):
                        for c in range(FC):
                            mm = pe.matmul(tail_ps[:, 0, t * P:(t + 1) * P], hT[:, c, t * P:(t + 1) * P],
                                           c2("w2")[:, c * D:(c + 1) * D], start=(c == 0), stop=(c == FC - 1))
                    mm.then_inc(ffn_made, 1)
                if r.tail:
                    pe.wait_ge(maxx_split, r.t)
                    if r.early:
                        pe.wait_ge(xT_copied, r.w)
                    elif r.self_:
                        pe.wait_ge(maxT_in[1], r.s)
                    else:
                        pe.wait_ge(kx_copied, r.t)
                        pe.wait_ge(vx_copied, r.t)
                    for t in range(QT):
                        mm = pe.transpose(prep_ps[:, t * P:(t + 1) * P],
                                          maxx_parts[:, t * QUADS:(t + 1) * QUADS, :], ident)
                    mm.then_inc(maxxT_made, 1)
                    expx_scores(0, r)
                if r.self_:
                    if r.tail:
                        pe.wait_ge(maxxT_in, r.t)
                    else:
                        pe.wait_ge(xT_copied, r.w)
                    max_transposes(2, r.s)
                if r.mid:
                    pe.wait_ge(x1_done, r.m)
                    if r.last:
                        pe.wait_ge(sum3_done, r.u)
                    for t in range(QT):
                        mm = pe.transpose(tail_ps[:, 0, t * P:(t + 1) * P], x1[:, t, :], ident)
                    mm.then_inc(x1T_made, 1)
                if r.self_:
                    max_scores(3, 0, r.s, max_done[2][1], r.s)
                if r.tail:
                    expx_scores(1, r)
                if r.early:
                    pe.wait_ge(xT_copied, r.w)
                    if r.self_:
                        pe.wait_ge(maxT_in[2], r.s)
                    pe.matmul(prep_ps[:, 0:S], c1("wq"), xT[:], start=True, stop=True)
                    pe.matmul(prep_ps[:, S:2 * S], c1("wk"), xT[:], start=True, stop=True).then_inc(qk_made, 1)
                if r.mid:
                    pe.wait_ge(x1T_copied, r.m)
                    pe.matmul(tail_ps[:, 1, 0:S], c2("wqx"), x1T[:], start=True, stop=True).then_inc(qx_made, 1)
                if r.self_:
                    if r.tail:
                        pe.wait_ge(expx_done[1], r.t)
                    exp_scores(2, 0, r.s, exp_done[1][1], r.s)
                    max_scores(3, 1, r.s, max_done[3][0], r.s)
                    pv(1, r.s, r.m)
                if r.tail:
                    pe.wait_ge(expx_done[0], r.t)
                    pe.wait_ge(expx_done[1], r.t)
                    pe.wait_ge(vx_copied, r.t)
                    if not r.mid:
                        pe.wait_ge(sum3_done, r.u)
                    for p in range(PAIRS):
                        h = p % HQ
                        mm = pe.matmul(tail_ps[STRIP * h:STRIP * (h + 1), 0, (p // HQ) * S:(p // HQ + 1) * S],
                                       vx_ones[:, p, :], probsx[:, p, :], start=True, stop=True,
                                       tile_position=(0, STRIP * h))
                    mm.then_inc(pvx_done, 1)
                if r.mid:
                    pe.wait_ge(ctx_loaded, r.m_32)
                    if r.early:
                        pe.wait_ge(qk_copied, r.w)
                    elif r.self_:
                        pe.wait_ge(maxT_in[2], r.s)
                    else:
                        pe.wait_ge(maxxT_in, r.t)
                    pe.transpose(prep_ps[:, 0:P], ctx_in[:], ident).then_inc(ctxT_made, 1)
                if r.self_:
                    exp_scores(2, 1, r.s, exp_done[2][0], r.s)
                if r.mid:
                    pe.wait_ge(ctxT_copied, r.m)
                    pe.matmul(prep_ps[:, 0:SC], c2("wkx"), ctxT2[:, 0:SC], start=True, stop=True)
                    pe.matmul(prep_ps[:, P:2 * P], ctxT2[:], c2("wvx"), start=True, stop=True).then_inc(kvx_made, 1)
                if r.tail:
                    pe.wait_ge(pvx_copied, r.t)
                    if r.mid:
                        pe.wait_ge(qx_copied, r.m)
                    for t in range(QT):
                        for j in range(2):
                            mm = pe.transpose(tail_ps[:, 1, (2 * t + j) * P:(2 * t + j + 1) * P],
                                              attvT[:, j, t * P:(t + 1) * P], ident)
                    mm.then_inc(pvxT_made, 1)
                if r.prep:
                    max_scores(0, 0, r.n, max_done[3][1], r.s)
                if r.self_:
                    if r.mid:
                        pe.wait_ge(kx_copied, r.m)
                        pe.wait_ge(vx_copied, r.m)
                    else:
                        pe.wait_ge(qk_copied, r.w)
                    max_transposes(3, r.s)
                    exp_scores(3, 0, r.s, exp_done[2][1], r.s)
                if r.tail:
                    pe.wait_ge(att2_done, r.t)
                    for t in range(QT):
                        mm = pe.transpose(tail_ps[:, 0, t * P:(t + 1) * P], att2[:, t, :], ident)
                    mm.then_inc(att2T_made, 1)
                if r.prep:
                    max_scores(0, 1, r.n, max_done[0][0], r.n)
                if r.self_:
                    pv(2, r.s, r.m)
                    exp_scores(3, 1, r.s, exp_done[3][0], r.s)
                if r.tail:
                    pe.wait_ge(att2T_copied, r.t)
                    for t in range(QT):
                        mm = pe.matmul(tail_ps[:, 1, t * P:(t + 1) * P], att2T[:, t * P:(t + 1) * P], c2("dense"),
                                       start=True, stop=True)
                    mm.then_inc(dense_made, 1)
                if r.prep:
                    if r.self_:
                        pe.wait_ge(maxT_in[3], r.s)
                    else:
                        pe.wait_ge(qk_copied, r.w)
                    max_transposes(0, r.n)

            pe.wait_ge(consts_ready, 1)
            pe.wait_ge(later_in, 16)
            iterations(pe, "pe", body)

        @block.scalar
        def _(act):
            def exp(g, half, done, previous):
                act.wait_ge(exp_ready[g][half], done)
                if half == 0:
                    used = done if g >= 2 else previous
                    if used:
                        act.wait_ge(pv_done[(g + 2) % QUADS], used)
                nc.scalar.activation(probs[:, g % 2, 2 * half:2 * half + 2, :, :], scores_kq[:], ACT.Exp
                                     ).then_inc(exp_done[g][half], 1)

            def maxT(g, done):
                act.wait_ge(maxT_made[g], done)
                nc.scalar.copy(slots[NROWS:NROWS + MROWS, g, 0, :].bitcast(F32R), prep_ps[0:MROWS, 0:S]
                               ).then_inc(maxT_in[g], 1)

            def pv_copy(half, done, previous):
                act.wait_ge(pv_done[2 * half + 1], done)
                if previous:
                    act.wait_ge(pvT_made, previous)
                nc.scalar.copy(ctxvT[:, 2 * half:2 * half + 2, :], pv_acc[:]).then_inc(pv_copied[half], 1)

            def body(r):
                if r.self_:
                    exp(0, 0, r.s, r.m)
                if r.mid:
                    pv_copy(1, r.m, r.t)
                if r.self_:
                    exp(0, 1, r.s, r.m)
                    maxT(1, r.s)
                if r.last:
                    act.wait_ge(x2T_made, r.u)
                    nc.scalar.copy(x2T[:], tail_ps[:, 0, 0:S]).then_inc(x2T_copied, 1)
                if r.self_:
                    exp(1, 0, r.s, r.m)
                if r.last:
                    act.wait_ge(h_made, r.u)
                    for c in range(FC):
                        ins = nc.scalar.activation(hT[:, c, :], tail_ps[:, c // 2, (c % 2) * S:(c % 2 + 1) * S],
                                                   ACT.Relu, bias=c2("b1")[:, c:c + 1])
                    ins.then_inc(h_copied, 1)
                if r.self_:
                    exp(1, 1, r.s, r.m)
                if r.early:
                    act.wait_ge(xT_made, r.w)
                    if r.n:
                        act.wait_ge(v_made, r.n)
                    nc.scalar.copy(xT[:], prep_ps[:, 0:S]).then_inc(xT_copied, 1)
                if r.tail:
                    act.wait_ge(maxxT_made, r.t)
                    for g in range(QUADS):
                        ins = nc.scalar.copy(qx_slots[NROWS:NROWS + MROWS, g, :].bitcast(F32R),
                                             prep_ps[STRIP * g:STRIP * g + MROWS, 0:S])
                    ins.then_inc(maxxT_in, 1)
                    act.wait_ge(expx_ready[0], r.t)
                    nc.scalar.activation(probsx[:, 0:4, :], scores_kq[:], ACT.Exp).then_inc(expx_done[0], 1)
                if r.self_:
                    maxT(2, r.s)
                if r.mid:
                    act.wait_ge(x1T_made, r.m)
                    nc.scalar.copy(x1T[:], tail_ps[:, 0, 0:S]).then_inc(x1T_copied, 1)
                if r.tail:
                    act.wait_ge(expx_ready[1], r.t)
                    nc.scalar.activation(probsx[:, 4:8, :], scores_kq[:], ACT.Exp).then_inc(expx_done[1], 1)
                if r.early:
                    act.wait_ge(qk_made, r.w)
                    if r.n:
                        act.wait_ge(rope_cos, r.n)
                        act.wait_ge(qk_swap_in, r.n_32)
                    nc.scalar.activation(qk[:, 0, :], prep_ps[:, 0:S], ACT.Identity, bias=c1("bq"))
                    nc.scalar.activation(qk[:, 1, :], prep_ps[:, S:2 * S], ACT.Identity, bias=c1("bk")).then_inc(qk_copied, 1)
                if r.mid:
                    act.wait_ge(qx_made, r.m)
                    if r.t:
                        act.wait_ge(qx_lo_done, r.t)
                    nc.scalar.activation(qx[:], tail_ps[:, 1, 0:S], ACT.Identity, bias=c2("bqx")).then_inc(qx_copied, 1)
                if r.self_:
                    exp(2, 0, r.s, r.m)
                    pv_copy(0, r.s, r.m)
                if r.tail:
                    act.wait_ge(pvx_done, r.t)
                    if r.u:
                        act.wait_ge(pvxT_made, r.u)
                    nc.scalar.copy(attvT[:], tail_ps[:, 0, :]).then_inc(pvx_copied, 1)
                if r.mid:
                    act.wait_ge(ctxT_made, r.m)
                    if r.t:
                        act.wait_ge(kvx_made, r.t)
                    nc.scalar.copy(ctxT2[:], prep_ps[:, 0:P]).then_inc(ctxT_copied, 1)
                if r.self_:
                    exp(2, 1, r.s, r.m)
                if r.self_:
                    maxT(3, r.s)
                    exp(3, 0, r.s, r.m)
                if r.tail:
                    act.wait_ge(att2T_made, r.t)
                    if r.u:
                        act.wait_ge(dense_made, r.u)
                    nc.scalar.copy(att2T[:], tail_ps[:, 0, 0:S]).then_inc(att2T_copied, 1)
                if r.self_:
                    exp(3, 1, r.s, r.m)
                if r.prep:
                    maxT(0, r.n)

            act.wait_ge(first_in, 16)
            act.wait_ge(later_in, 16)
            act.wait_ge(zeroed, 3)
            iterations(act, "act", body)

        @block.vector
        def _(dve):
            nc.vector.memset(slots[NROWS:P, :, 0, :], 0.0)
            nc.vector.memset(slots[NROWS:P, :, 1, :], 1.0)
            nc.vector.memset(qx_slots[NROWS:P, :, :], 0.0)
            nc.vector.memset(kx_slots[NROWS:P, :, :], 1.0)
            nc.vector.memset(minus_half[:], -0.5)
            nc.vector.memset(y[:], 0.0).then_inc(stored, 16)
            nc.vector.memset(maxx_parts[:], 0.0).then_inc(zeroed, 1)
            nc.vector.memset(v_ones[:], 0.0).then_inc(zeroed, 1)
            nc.vector.memset(vx_ones[:], 0.0).then_inc(zeroed, 1)
            dve.wait_ge(zeroed, 3)
            nc.vector.memset(v_ones[:, :, :, HD:HD + 1], 1.0).then_inc(mask_step, 1)
            nc.vector.memset(vx_ones[0:SC, :, HD:HD + 1], 1.0)
            nc.vector.memset(vx_ones[SC:P, :, 16 + HD:16 + HD + 1], 1.0)
            dve.wait_ge(later_in, 16)
            nc.vector.tensor_copy(key_of_row[:].bitcast(F32R), c2("key_of_row"))
            nc.vector.tensor_scalar(mask_neg[:], c2("mask"), MASK_SCALE, None, ALU.mult).then_inc(mask_step, 1)
            dve.wait_ge(mask_step, 2)
            nc.vector.tensor_copy(mask_hi[:].bitcast(F32R), mask_neg[:])
            nc.vector.tensor_copy(mask_parts[0:SC, :].bitcast(F32R), mask_neg[0:SC, :]).then_inc(mask_step, 1)
            dve.wait_ge(mask_step, 3)
            nc.vector.tensor_tensor(mask_parts[SC:P, :].bitcast(F32R), mask_neg[SC:P, :], mask_hi[SC:P, :], ALU.subtract
                                    ).then_inc(consts_ready, 1)

            def reduce(g, t, done):
                dve.wait_ge(max_ready[g][t], done)
                nc.vector.tensor_reduce(neg_max[:, g, t, :], scores_qk[:].rearrange("p (h k) -> p h k", k=S), AX.X,
                                        ALU.max, negate=True).then_inc(max_done[g][t], 1)

            def split_max(g, done):
                dve.wait_ge(max_done[g][1], done)
                nc.vector.tensor_copy(max_parts[:, g, :, 0:HQ].bitcast(F32R), neg_max[:, g, :, :]).then_inc(max_hi_done[g], 1)
                dve.wait_ge(max_hi_done[g], done)
                nc.vector.tensor_tensor(max_parts[:, g, :, HQ:MROWS].bitcast(F32R), neg_max[:, g, :, :],
                                        max_parts[:, g, :, 0:HQ], ALU.subtract).then_inc(max_split[g], 1)

            def norm_stats(n, src, src_done, done):
                dve.wait_ge(src_done, done)
                for t in range(QT):
                    ins = nc.vector.bn_stats(stats[:, n, t, :], src[:, t, :])
                ins.then_inc(stats_done[n], 1)
                fixed_wait(dve)
                dve.wait_ge(stats_done[n], done)
                for t in range(QT):
                    ins = nc.vector.bn_aggr(mean_var[:, n, t, :], stats[:, n, t, :])
                ins.then_inc(aggr_done[n], 1)
                dve.wait_ge(aggr_done[n], done)
                nc.vector.tensor_scalar(var_eps[:, n, :], mean_var[:, n, :, 1], EPS, None, ALU.add).then_inc(var_done[n], 1)

            def normalize(n, src, out, out_done, done):
                dve.wait_ge(rstd_done[n], done)
                for t in range(QT):
                    ins = nc.vector.tensor_scalar(out[:, t, :], src[:, t, :], mean_var[:, n, t, 0:1], rstd[:, n, t:t + 1],
                                                  ALU.subtract, ALU.mult)
                ins.then_inc(out_done, 1)

            def body(r):
                if r.self_:
                    reduce(1, 0, r.s)
                if r.last:
                    normalize(1, sum2, x2, x2_done, r.u)
                if r.self_:
                    reduce(1, 1, r.s)
                    split_max(1, r.s)
                if r.prep:
                    dve.wait_ge(v_made, r.n)
                    if r.s:
                        dve.wait_ge(v_placed, r.s)
                    nc.vector.tensor_copy(v_rows[:], prep_ps[:, 0:S].rearrange("p (t d) -> p t d", t=QT)).then_inc(v_copied, 1)
                if r.mid:
                    dve.wait_ge(pvT_made, r.m)
                    pvT = tail_ps[:].rearrange("p t (h c) -> p (t h) c", c=STRIP)
                    nc.vector.reciprocal(recip1[:], pvT[:, :, HD]).then_inc(recip1_done, 1)
                    dve.wait_ge(recip1_done, r.m)
                    nc.vector.tensor_tensor(att1[:].rearrange("p t (h c) -> p (t h) c", c=HD), pvT[:, :, 0:HD],
                                            recip1[:].rearrange("p (h o) -> p h o", o=1).to_broadcast([P, QT * H, HD]),
                                            ALU.mult).then_inc(att1_done, 1)
                if r.tail:
                    dve.wait_ge(maxx_ready[0], r.t)
                    nc.vector.tensor_reduce(neg_maxx[:, 0:QUADS, :], scores_qk[:].rearrange("p (h k) -> p h k", k=SC), AX.X,
                                            ALU.max, negate=True).then_inc(maxx_done[0], 1)
                if r.mid:
                    dve.wait_ge(att1_done, r.m)
                    dve.wait_ge(xres_loaded, r.m_16)
                    nc.vector.tensor_tensor(sum1[:], att1[:], x_res[:], ALU.add).then_inc(sum1_done, 1)
                    norm_stats(0, sum1, sum1_done, r.m)
                if r.prep:
                    dve.wait_ge(rope_done, r.n)
                    for g in range(QUADS):
                        if r.s:
                            dve.wait_ge(slots_in[g], r.s_48)
                    nc.vector.tensor_copy(qk_parts[:, 0:4:2, :].bitcast(F32R), qk_rope[:]).then_inc(qk_hi_done, 1)
                if r.tail:
                    dve.wait_ge(maxx_ready[1], r.t)
                    nc.vector.tensor_reduce(neg_maxx[:, QUADS:2 * QUADS, :], scores_qk[:].rearrange("p (h k) -> p h k", k=SC),
                                            AX.X, ALU.max, negate=True).then_inc(maxx_done[1], 1)
                    dve.wait_ge(maxx_done[1], r.t)
                    if r.u:
                        dve.wait_ge(maxxT_made, r.u)
                    nc.vector.tensor_copy(maxx_parts[:, :, 0:HQ].bitcast(F32R), neg_maxx[:]).then_inc(maxx_hi_done, 1)
                    dve.wait_ge(maxx_hi_done, r.t)
                    nc.vector.tensor_tensor(maxx_parts[:, :, HQ:MROWS].bitcast(F32R), neg_maxx[:], maxx_parts[:, :, 0:HQ],
                                            ALU.subtract).then_inc(maxx_split, 1)
                if r.self_:
                    reduce(2, 0, r.s)
                if r.mid:
                    if r.t:
                        dve.wait_ge(x1b_done, r.t)
                        dve.wait_ge(x1T_made, r.t)
                    normalize(0, sum1, x1, x1_done, r.m)
                if r.self_:
                    reduce(2, 1, r.s)
                    split_max(2, r.s)
                if r.last:
                    dve.wait_ge(ffn_made, r.u)
                    dve.wait_ge(x2b_done, r.u)
                    nc.vector.tensor_tensor(sum3[:], tail_ps[:, 0, 0:S].rearrange("p (t d) -> p t d", t=QT), x2_bias[:],
                                            ALU.add).then_inc(sum3_done, 1)
                    norm_stats(2, sum3, sum3_done, r.u)
                if r.self_:
                    reduce(3, 0, r.s)
                if r.mid:
                    dve.wait_ge(qx_copied, r.m)
                    if r.t:
                        dve.wait_ge(qx_out, r.t_16)
                    nc.vector.tensor_copy(qx_parts[:, 0, :].bitcast(F32R), qx[:]).then_inc(qx_hi_done, 1)
                if r.last:
                    dve.wait_ge(stored, r.u_16)
                    normalize(2, sum3, y, y_done, r.u)
                if r.self_:
                    reduce(3, 1, r.s)
                    split_max(3, r.s)
                if r.mid:
                    dve.wait_ge(kvx_made, r.m)
                    if r.t:
                        dve.wait_ge(kx_lo_done, r.t)
                    nc.vector.tensor_scalar(kx[:], prep_ps[:, 0:SC], c2("bkx"), KSCALE, ALU.add, ALU.mult).then_inc(kx_copied, 1)
                    if r.t:
                        dve.wait_ge(pvx_done, r.t)
                    for j in range(2):
                        rows = slice(j * SC, (j + 1) * SC)
                        ins = nc.vector.tensor_tensor(
                            vx_ones[rows, :, 16 * j:16 * j + HD],
                            prep_ps[rows, P:2 * P].rearrange("p (a j c) -> p a j c", j=2, c=HD)[:, :, j, :],
                            c2("bvx")[rows, :].rearrange("p (a j c) -> p a j c", j=2, c=HD)[:, :, j, :], ALU.add)
                    ins.then_inc(vx_copied, 1)
                    dve.wait_ge(kx_copied, r.m)
                    if r.t:
                        dve.wait_ge(kx_out, r.t_16)
                    nc.vector.tensor_copy(kx_parts[:, 0, :].bitcast(F32R), kx[:]).then_inc(kx_hi_done, 1)
                    dve.wait_ge(kx_hi_done, r.m)
                    nc.vector.tensor_tensor(kx_parts[:, 1, :].bitcast(F32R), kx[:], kx_parts[:, 0, :], ALU.subtract
                                            ).then_inc(kx_lo_done, 1)
                if r.tail:
                    dve.wait_ge(pvxT_made, r.t)
                    pvxT = tail_ps[:, 1, :].rearrange("p (h c) -> p h c", c=16)
                    nc.vector.reciprocal(recip2[:], pvxT[:, :, HD]).then_inc(recip2_done, 1)
                    dve.wait_ge(recip2_done, r.t)
                    nc.vector.tensor_tensor(att2[:].rearrange("p t (h c) -> p (t h) c", c=HD), pvxT[:, :, 0:HD],
                                            recip2[:].rearrange("p (h o) -> p h o", o=1).to_broadcast([P, QT * H, HD]),
                                            ALU.mult).then_inc(att2_done, 1)
                if r.prep:
                    reduce(0, 0, r.n)
                    reduce(0, 1, r.n)
                    split_max(0, r.n)
                if r.tail:
                    dve.wait_ge(dense_made, r.t)
                    dve.wait_ge(x1b_done, r.t)
                    nc.vector.tensor_tensor(sum2[:], tail_ps[:, 1, 0:S].rearrange("p (t d) -> p t d", t=QT), x1_bias[:],
                                            ALU.add).then_inc(sum2_done, 1)
                    norm_stats(1, sum2, sum2_done, r.t)

            dve.wait_ge(first_in, 16)
            iterations(dve, "dve", body)

        @block.gpsimd
        def _(pool):
            def inverse_std(n, done):
                pool.wait_ge(var_done[n], done)
                nc.gpsimd.tensor_tensor(rstd[:, n, :], var_eps[:, n, :], minus_half[:], ALU.pow).then_inc(rstd_done[n], 1)

            row_head = c1("head_of_row").rearrange("p (h o) -> p h o", o=1)

            def diagonal(g, loaded, used):
                pool.wait_ge(slots_in[g], loaded)
                if used:
                    pool.wait_ge(exp_ready[g][1], used)
                nc.gpsimd.tensor_tensor(k_diag[:, g, :, :].bitcast(F32R),
                                        slots[:, g, 1:2, :].to_broadcast([P, HQ, S]),
                                        row_head.to_broadcast([P, HQ, S]), ALU.mult).then_inc(diag_done[g], 1)

            def body(r):
                if r.self_:
                    pool.wait_ge(v_copied, r.s)
                    if r.m:
                        pool.wait_ge(pv_done[3], r.m)
                    for t in range(QT):
                        ins = nc.gpsimd.tensor_tensor(v_ones[:, t, :, 0:HD], v_rows[:, t, :].rearrange("p (h c) -> p h c", c=HD),
                                                      c1("bv").rearrange("p (h c) -> p h c", c=HD), ALU.add)
                    ins.then_inc(v_placed, 1)
                    diagonal(3, r.s_48, r.m)
                if r.last:
                    pool.wait_ge(x2_done, r.u)
                    nc.gpsimd.tensor_tensor(x2_bias[:], x2[:], c2("b2").rearrange("p (o d) -> p o d", o=1)
                                            .to_broadcast([P, QT, D]), ALU.add).then_inc(x2b_done, 1)
                if r.mid:
                    inverse_std(0, r.m)
                if r.prep:
                    pool.wait_ge(qk_hi_done, r.n)
                    nc.gpsimd.tensor_tensor(qk_parts[:, 1:4:2, :].bitcast(F32R), qk_rope[:], qk_parts[:, 0:4:2, :],
                                            ALU.subtract).then_inc(qk_lo_done, 1)
                    diagonal(0, r.n_48, r.s)
                if r.last:
                    inverse_std(2, r.u)
                if r.mid:
                    pool.wait_ge(qx_hi_done, r.m)
                    nc.gpsimd.tensor_tensor(qx_parts[:, 1, :].bitcast(F32R), qx[:], qx_parts[:, 0, :], ALU.subtract
                                            ).then_inc(qx_lo_done, 1)
                if r.prep:
                    diagonal(1, r.n_48, r.s)
                if r.early:
                    pool.wait_ge(qk_copied, r.w)
                    if r.n:
                        pool.wait_ge(rope_done, r.n)
                    nc.gpsimd.tensor_tensor(qk_cos[:], qk[:], c1("cos").rearrange("p (j c) -> p j c", j=2), ALU.mult
                                            ).then_inc(rope_cos, 1)
                    pool.wait_ge(qk_swap_in, r.w_32)
                    nc.gpsimd.tensor_tensor(qk_sin[:], qk_swapped[:], c1("sin").rearrange("p (j c) -> p j c", j=2), ALU.mult
                                            ).then_inc(rope_sin, 1)
                    pool.wait_ge(rope_cos, r.w)
                    pool.wait_ge(rope_sin, r.w)
                    if r.n:
                        pool.wait_ge(qk_lo_done, r.n)
                    nc.gpsimd.tensor_tensor(qk_rope[:], qk_cos[:], qk_sin[:], ALU.add).then_inc(rope_done, 1)
                if r.prep:
                    diagonal(2, r.n_48, r.s)
                if r.tail:
                    inverse_std(1, r.t)
                if r.mid:
                    pool.wait_ge(kx_slots_in, r.m_48)
                    if r.t:
                        pool.wait_ge(expx_ready[1], r.t)
                    for g in range(QUADS):
                        ins = nc.gpsimd.tensor_tensor(kx_diag[:, g, :, :].bitcast(F32R),
                                                      kx_slots[:, g:g + 1, :].to_broadcast([P, HQ, SC]),
                                                      row_head.to_broadcast([P, HQ, SC]), ALU.mult)
                    ins.then_inc(kx_diag_done, 1)
                    pool.wait_ge(x1_done, r.m)
                    if r.t:
                        pool.wait_ge(sum2_done, r.t)
                    nc.gpsimd.tensor_tensor(x1_bias[:], x1[:], c2("dense_b").rearrange("p (o d) -> p o d", o=1)
                                            .to_broadcast([P, QT, D]), ALU.add).then_inc(x1b_done, 1)

            pool.wait_ge(first_in, 16)
            pool.wait_ge(later_in, 16)
            pool.wait_ge(zeroed, 3)
            pool.wait_ge(consts_ready, 1)
            iterations(pool, "pool", body)


def shape_constants():
    import numpy as np

    row = np.arange(P)
    dim = row % HD
    inv = np.power(np.float32(10000.0), -2.0 * np.arange(HD // 2, dtype=np.float32) / np.float32(HD)).astype(np.float32)
    angle = (np.arange(S, dtype=np.float32)[None, :] * inv[dim // 2][:, None]).astype(np.float32)
    sign = np.where(dim % 2 == 0, -1.0, 1.0)[:, None]
    scale = np.array([1.0, KSCALE])[None, :, None]
    cos = (np.cos(angle.astype(np.float64))[:, None, :] * scale).reshape(P, 2 * S)
    sin = ((sign * np.sin(angle.astype(np.float64)))[:, None, :] * scale).reshape(P, 2 * S)
    head = np.where(row < NROWS, (row % QROWS) // HD, np.where(row < NROWS + MROWS, row % HQ, -1))
    return {
        "ident": np.eye(P, dtype=np.float32),
        "cos": cos.astype(np.float32),
        "sin": sin.astype(np.float32),
        "head_of_row": (head[:, None] == np.arange(HQ)[None, :]).astype(np.float32),
        "key_of_row": (row[:, None] % SC == np.arange(8 * SC)[None, :] % SC).astype(np.float32),
    }


def kernel(**inputs):
    import numpy as np
    import concourse.bacc as bacc
    from concourse.bass_utils import run_bass_kernel_spmd

    a = {k: np.asarray(v) for k, v in inputs.items()}
    column = lambda v: v.reshape(-1, P).T
    every_row = lambda v: np.broadcast_to(v[None, :], (P, v.shape[0]))
    maskT = a["mask_1x1xSxS2_fk1"][0, 0].T
    parts = dict(shape_constants())
    parts.update(
        wq=a["L0_attn_Wq"], wk=a["L0_attn_Wk"], wv=a["L0_attn_Wv"],
        bq=column(a["L0_attn_bq"]), bk=column(a["L0_attn_bk"]), bv=every_row(a["L0_attn_bv"]),
        wqx=a["L0_xattn_wq_w"].T, wkx=a["L0_xattn_wk_w"].T, wvx=a["L0_xattn_wv_w"].T, dense=a["L0_xattn_dense_w"].T,
        w1=a["L0_ffn_W1"], w2=a["L0_ffn_W2"].reshape(FC, P, D).transpose(1, 0, 2).reshape(P, FC * D),
        bqx=column(a["L0_xattn_wq_b"]), bkx=column(a["L0_xattn_wk_b"]), b1=column(a["L0_ffn_b1"]),
        bvx=every_row(a["L0_xattn_wv_b"]), dense_b=every_row(a["L0_xattn_dense_b"]), b2=every_row(a["L0_ffn_b2"]),
        mask=np.concatenate([maskT, maskT], axis=0),
    )
    arrays = {
        "x": np.ascontiguousarray(a["x"]),
        "ctx": np.ascontiguousarray(a["ctx_1024"]),
        "first": np.ascontiguousarray(np.concatenate([parts[n] for n, _ in FIRST], axis=1)),
        "later": np.ascontiguousarray(np.concatenate([parts[n] for n, _ in LATER], axis=1)),
    }
    nc = bacc.Bacc("TRN2", target_bir_lowering=False, num_devices=1)
    args = [nc.dram_tensor(n, v.shape, mybir.dt.from_np(v.dtype), kind="ExternalInput").ap() for n, v in arrays.items()]
    out = nc.dram_tensor("out", (B, S, D), F32, kind="ExternalOutput").ap()
    build(nc, *args, out)
    return run_bass_kernel_spmd(nc, [arrays], core_ids=[0]).results[0]["out"]
```

```python
from contextlib import ExitStack

import concourse.bass as bass
from concourse import mybir

F32 = mybir.dt.float32
F32R = mybir.dt.float32r
ALU = mybir.AluOpType
ACT = mybir.ActivationFunctionType
AX = mybir.AxisListType

P = 128
B, S, D = 8, 256, 128
SC = 64
H, HD = 16, 8
FF = 512
QT = S // P
QUADS, HQ = 4, 4
PAIRS = H // 2
FC = FF // P
STRIP = 32
QROWS = HQ * HD
NROWS = 3 * QROWS
MROWS = 2 * HQ
EPS = 1e-5
MASK_SCALE = -1e9
KSCALE = HD ** -0.5

FIRST = [("ident", P), ("wq", D), ("wk", D), ("bq", 1), ("bk", 1)]
SECOND = [("cos", 2 * S), ("sin", 2 * S), ("head_of_row", HQ), ("wv", D), ("bv", D)]
LATER = [("wqx", D), ("wkx", D), ("wvx", D), ("dense", D), ("w1", FF), ("w2", FC * D), ("bqx", 1), ("bkx", 1),
         ("b1", FC), ("bvx", D), ("dense_b", D), ("b2", D), ("mask", S), ("key_of_row", 8 * SC)]


def columns(fields):
    at, n = {}, 0
    for name, width in fields:
        at[name] = (n, width)
        n += width
    return at, n


FIRST_AT, FIRST_N = columns(FIRST)
SECOND_AT, SECOND_N = columns(SECOND)
LATER_AT, LATER_N = columns(LATER)


def build(nc, x_d, ctx_d, first_d, second_d, later_d, out_d):
    with ExitStack() as ctx:
        def sb(name, shape):
            return ctx.enter_context(nc.sbuf_tensor(name, shape, F32))

        def psum(name, shape):
            return ctx.enter_context(nc.psum_tensor(name, shape, F32))

        def sem(name):
            return ctx.enter_context(nc.semaphore(name))

        def sems(name, n):
            return [sem(f"{name}{j}") for j in range(n)]

        qx_scratch = nc.dram_tensor("qx_scratch", [P, 2, S], F32, kind="Internal").ap()
        kx_scratch = nc.dram_tensor("kx_scratch", [P, 2, SC], F32, kind="Internal").ap()

        first = sb("first_sb", [P, FIRST_N])
        second = sb("second_sb", [P, SECOND_N])
        later = sb("later_sb", [P, LATER_N])

        def const(name):
            for array, at in ((first, FIRST_AT), (second, SECOND_AT), (later, LATER_AT)):
                if name in at:
                    return array[:, at[name][0]:at[name][0] + at[name][1]]
            raise KeyError(name)

        x_in = sb("x_in", [P, QT, D])
        x_res = sb("x_res", [P, QT, D])
        ctx_in = sb("ctx_in", [P, D])
        xT = sb("xT", [P, S])
        qk = sb("qk", [P, 2, S])
        qk_swapped = sb("qk_swapped", [P, 2, S])
        qk_cos = sb("qk_cos", [P, 2, S])
        qk_sin = sb("qk_sin", [P, 2, S])
        qk_rope = sb("qk_rope", [P, 2, S])
        qk_parts = sb("qk_parts", [P, 4, S])
        slots = sb("slots", [P, QUADS, 2, S])
        k_diag = sb("k_diag", [P, QUADS, HQ, S])
        v_rows = sb("v_rows", [P, QT, D])
        v_ones = sb("v_ones", [P, QT, H, STRIP])
        neg_max = sb("neg_max", [P, QUADS, QT, HQ])
        max_parts = sb("max_parts", [P, QUADS, QT, P // QT])
        probs = sb("probs", [P, 2, HQ, QT, S])
        ctxvT = sb("ctxvT", [P, QUADS, S])
        recip1 = sb("recip1", [P, QT * H])
        att1 = sb("att1", [P, QT, D])
        sum1 = sb("sum1", [P, QT, D])
        x1 = sb("x1", [P, QT, D])
        x1_bias = sb("x1_bias", [P, QT, D])
        x1T = sb("x1T", [P, S])
        qx = sb("qx", [P, S])
        qx_parts = sb("qx_parts", [P, 2, S])
        qx_slots = sb("qx_slots", [P, QUADS, S])
        ctxT2 = sb("ctxT2", [P, 2 * SC])
        kx = sb("kx", [P, SC])
        kx_parts = sb("kx_parts", [P, 2, SC])
        kx_slots = sb("kx_slots", [P, QUADS, SC])
        kx_diag = sb("kx_diag", [P, QUADS, HQ, SC])
        vx_ones = sb("vx_ones", [P, PAIRS, STRIP])
        neg_maxx = sb("neg_maxx", [P, QT * QUADS, HQ])
        maxx_parts = sb("maxx_parts", [P, QT * QUADS, STRIP])
        probsx = sb("probsx", [P, PAIRS, S])
        attvT = sb("attvT", [P, 2, S])
        recip2 = sb("recip2", [P, QT * H])
        att2 = sb("att2", [P, QT, D])
        att2T = sb("att2T", [P, S])
        sum2 = sb("sum2", [P, QT, D])
        x2 = sb("x2", [P, QT, D])
        x2_bias = sb("x2_bias", [P, QT, D])
        x2T = sb("x2T", [P, S])
        hT = sb("hT", [P, FC, S])
        sum3 = sb("sum3", [P, QT, D])
        y = sb("y", [P, QT, D])
        stats = sb("stats", [P, 3, QT, 6])
        mean_var = sb("mean_var", [P, 3, QT, 2])
        var_eps = sb("var_eps", [P, 3, QT])
        rstd = sb("rstd", [P, 3, QT])
        minus_half = sb("minus_half", [P, QT])
        mask_neg = sb("mask_neg", [P, S])
        mask_parts = sb("mask_parts", [P, S])
        mask_hi = sb("mask_hi", [P, S])
        key_of_row = sb("key_of_row", [P, 8 * SC])

        scores_qk = psum("scores_qk", [P, 1024])
        scores_kq = psum("scores_kq", [P, 1024])
        pv_acc = psum("pv_acc", [P, 2, S])
        prep_ps = psum("prep_ps", [P, 512])
        tail_ps = psum("tail_ps", [P, 2, 512])

        first_in, second_in, later_in = sem("first_in"), sem("second_in"), sem("later_in")
        zeroed, consts_ready = sem("zeroed"), sem("consts_ready")
        mask_step = sem("mask_step")
        x_loaded, xres_loaded, ctx_loaded = sem("x_loaded"), sem("xres_loaded"), sem("ctx_loaded")
        xT_made, xT_copied = sem("xT_made"), sem("xT_copied")
        qk_made, qk_copied, qk_swap_in = sem("qk_made"), sem("qk_copied"), sem("qk_swap_in")
        rope_cos, rope_sin, rope_done = sem("rope_cos"), sem("rope_sin"), sem("rope_done")
        qk_hi_done, qk_lo_done = sem("qk_hi_done"), sem("qk_lo_done")
        v_made, v_copied, v_placed = sem("v_made"), sem("v_copied"), sem("v_placed")
        slots_in, diag_done = sems("slots_in", QUADS), sems("diag_done", QUADS)
        max_ready = [sems(f"max_ready{g}_", QT) for g in range(QUADS)]
        max_done = [sems(f"max_done{g}_", QT) for g in range(QUADS)]
        max_hi_done, max_split = sems("max_hi_done", QUADS), sems("max_split", QUADS)
        maxT_made, maxT_in = sems("maxT_made", QUADS), sems("maxT_in", QUADS)
        exp_ready = [sems(f"exp_ready{g}_", 2) for g in range(QUADS)]
        exp_done = [sems(f"exp_done{g}_", 2) for g in range(QUADS)]
        pv_done = sems("pv_done", QUADS)
        pv_copied = sems("pv_copied", 2)
        pvT_made = sem("pvT_made")
        recip1_done, att1_done, sum1_done = sem("recip1_done"), sem("att1_done"), sem("sum1_done")
        stats_done, aggr_done, var_done, rstd_done = (sems(n, 3) for n in ("stats_done", "aggr_done", "var_done", "rstd_done"))
        x1_done, x1b_done, x1T_made, x1T_copied = sem("x1_done"), sem("x1b_done"), sem("x1T_made"), sem("x1T_copied")
        qx_made, qx_copied, qx_hi_done, qx_lo_done = sem("qx_made"), sem("qx_copied"), sem("qx_hi_done"), sem("qx_lo_done")
        qx_out, qx_slots_in = sem("qx_out"), sem("qx_slots_in")
        ctxT_made, ctxT_copied = sem("ctxT_made"), sem("ctxT_copied")
        kx_made, vx_made, kx_copied, vx_copied = sem("kx_made"), sem("vx_made"), sem("kx_copied"), sem("vx_copied")
        kx_hi_done, kx_lo_done, kx_out, kx_slots_in = sem("kx_hi_done"), sem("kx_lo_done"), sem("kx_out"), sem("kx_slots_in")
        kx_diag_done = sem("kx_diag_done")
        maxx_ready, maxx_done = sems("maxx_ready", QT), sems("maxx_done", QT)
        maxx_hi_done, maxx_split, maxxT_made, maxxT_in = sem("maxx_hi_done"), sem("maxx_split"), sem("maxxT_made"), sem("maxxT_in")
        expx_ready, expx_done = sems("expx_ready", 2), sems("expx_done", 2)
        pvx_done, pvx_copied, pvxT_made = sem("pvx_done"), sem("pvx_copied"), sem("pvxT_made")
        recip2_done, att2_done, att2T_made, att2T_copied = sem("recip2_done"), sem("att2_done"), sem("att2T_made"), sem("att2T_copied")
        dense_made, sum2_done, x2_done, x2b_done = sem("dense_made"), sem("sum2_done"), sem("x2_done"), sem("x2b_done")
        x2T_made, x2T_copied, h_made, h_copied = sem("x2T_made"), sem("x2T_copied"), sem("h_made"), sem("h_copied")
        ffn_made, sum3_done, y_done, stored = sem("ffn_made"), sem("sum3_done"), sem("y_done"), sem("stored")

        def fixed_wait(eng):
            eng.wait_ge(first_in, 16)

        FIRST_LOOPED, END_LOOPED = 3, B - 2

        class Counts:

            def __init__(self, at):
                self.w, self.n, self.s = at("w", 3, 1), at("n", 2, 1), at("s", 1, 1)
                self.m, self.t, self.u = at("m", 0, 1), at("t", -1, 1), at("u", -2, 1)

            def dma(self, at):
                self.w_16, self.w_32, self.n_32 = at("w_16", 3, 16), at("w_32", 3, 32), at("n_32", 2, 32)
                self.n_48, self.s_48 = at("n_48", 2, 48), at("s_48", 1, 48)
                self.m_16, self.m_32, self.m_48 = at("m_16", 0, 16), at("m_32", 0, 32), at("m_48", 0, 48)
                self.t_16, self.t_48, self.u_16 = at("t_16", -1, 16), at("t_48", -1, 48), at("u_16", -2, 16)
                return self

        def peeled(e):
            number = lambda name, k, unit: min(max(0, e + k), B) * unit
            r = Counts(number).dma(number)
            r.e = e
            r.early, r.prep, r.self_ = e + 2 < B, 0 <= e + 1 < B, 0 <= e < B
            r.mid, r.tail, r.last = 0 <= e - 1 < B, 0 <= e - 2 < B, 0 <= e - 3 < B
            r.starts_early, r.starts_prep, r.starts_self, r.starts_mid = e == -2, e == -1, e == 0, e == 1
            return r

        def iterations(eng, name, used, body):
            for e in range(-2, FIRST_LOOPED):
                body(peeled(e))
            registers = []

            def register(role, k, unit):
                if role not in used.split():
                    return None
                reg = eng.alloc_register(f"{name}_{role}_runs")
                eng.reg_mov(reg, (FIRST_LOOPED + k) * unit)
                registers.append((reg, unit))
                return reg

            r = Counts(register).dma(register)
            r.early = r.prep = r.self_ = r.mid = r.tail = r.last = True
            r.starts_early = r.starts_prep = r.starts_self = r.starts_mid = False
            with eng.Fori(FIRST_LOOPED, END_LOOPED) as e:
                r.e = e
                body(r)
                for reg, unit in registers:
                    eng.reg_add(reg, reg, unit)
            for e in range(END_LOOPED, B + 3):
                body(peeled(e))

        row_head = const("head_of_row").rearrange("p (h o) -> p h o", o=1)

        def rope_cosine(eng, ops, r):
            eng.wait_ge(qk_copied, r.n)
            if r.s:
                eng.wait_ge(rope_done, r.s)
            ops.tensor_tensor(qk_cos[:], qk[:], const("cos").rearrange("p (j c) -> p j c", j=2), ALU.mult
                                    ).then_inc(rope_cos, 1)

        def rope_sine(eng, ops, r):
            eng.wait_ge(qk_swap_in, r.n_32)
            ops.tensor_tensor(qk_sin[:], qk_swapped[:], const("sin").rearrange("p (j c) -> p j c", j=2), ALU.mult
                                    ).then_inc(rope_sin, 1)

        def rope_sum(eng, ops, r):
            eng.wait_ge(rope_cos, r.n)
            eng.wait_ge(rope_sin, r.n)
            if r.s:
                eng.wait_ge(qk_lo_done, r.s)
            ops.tensor_tensor(qk_rope[:], qk_cos[:], qk_sin[:], ALU.add).then_inc(rope_done, 1)

        def qk_low(eng, ops, r):
            eng.wait_ge(qk_hi_done, r.n)
            ops.tensor_tensor(qk_parts[:, 1:4:2, :].bitcast(F32R), qk_rope[:], qk_parts[:, 0:4:2, :],
                                    ALU.subtract).then_inc(qk_lo_done, 1)

        def diagonal(eng, ops, g, loaded, used):
            eng.wait_ge(slots_in[g], loaded)
            if used:
                eng.wait_ge(exp_ready[g][1], used)
            ops.tensor_tensor(k_diag[:, g, :, :].bitcast(F32R), slots[:, g, 1:2, :].to_broadcast([P, HQ, S]),
                              row_head.to_broadcast([P, HQ, S]), ALU.mult).then_inc(diag_done[g], 1)

        block = ctx.enter_context(nc.Block())

        @block.sync
        def _(sp):
            sp.dma_start(first[:], first_d).then_inc(first_in, 16)

            def slot_loads(g, made, used):
                sp.wait_ge(qk_lo_done, made)
                if used:
                    sp.wait_ge(exp_ready[g][1], used)
                if used:
                    sp.wait_ge(diag_done[g], used)
                for s, (qp, kp) in enumerate(((0, 2), (0, 3), (1, 2))):
                    sp.dma_start(slots[QROWS * s:QROWS * (s + 1), g, :, :],
                                 qk_parts[QROWS * g:QROWS * (g + 1), qp:kp + 1:kp - qp, :]).then_inc(slots_in[g], 16)

            def body(r):
                if r.mid:
                    fixed_wait(sp)
                    if r.t:
                        sp.wait_ge(ctxT_made, r.t)
                    for j in range(2):
                        sp.dma_start(ctx_in[j * SC:(j + 1) * SC, :], ctx_d[r.e - 1]).then_inc(ctx_loaded, 16)
                    fixed_wait(sp)
                    if r.t:
                        sp.wait_ge(sum1_done, r.t)
                    sp.dma_start(x_res[:], x_d[r.e - 1].rearrange("(t p) d -> p t d", p=P)).then_inc(xres_loaded, 16)
                if r.early:
                    if r.n:
                        fixed_wait(sp)
                        sp.wait_ge(xT_made, r.n)
                    sp.dma_start(x_in[:], x_d[r.e + 2].rearrange("(t p) d -> p t d", p=P)).then_inc(x_loaded, 16)
                if r.starts_early:
                    sp.dma_start(second[:], second_d).then_inc(second_in, 16)
                    sp.dma_start(later[:], later_d).then_inc(later_in, 16)
                if r.self_:
                    slot_loads(3, r.s, r.m)
                if r.prep:
                    slot_loads(0, r.n, r.s)
                    slot_loads(1, r.n, r.s)
                if r.mid:
                    sp.wait_ge(kx_lo_done, r.m)
                    if r.t:
                        sp.wait_ge(kx_slots_in, r.t_48)
                    sp.dma_start(kx_scratch, kx_parts[:]).then_inc(kx_out, 16)
                    sp.wait_ge(kx_out, r.m_16)
                    if r.t:
                        sp.wait_ge(kx_diag_done, r.t)
                    for s, part in enumerate((0, 1, 0)):
                        sp.dma_start(kx_slots[QROWS * s:QROWS * (s + 1), :, :],
                                     kx_scratch[:, part, :].rearrange("(g r) c -> r g c", g=QUADS)).then_inc(kx_slots_in, 16)
                    sp.wait_ge(qx_lo_done, r.m)
                    if r.t:
                        sp.wait_ge(qx_slots_in, r.t_48)
                    sp.dma_start(qx_scratch, qx_parts[:]).then_inc(qx_out, 16)
                if r.prep:
                    slot_loads(2, r.n, r.s)
                if r.mid:
                    sp.wait_ge(qx_out, r.m_16)
                    if r.t:
                        sp.wait_ge(expx_ready[1], r.t)
                    for s, part in enumerate((0, 0, 1)):
                        sp.dma_start(qx_slots[QROWS * s:QROWS * (s + 1), :, :],
                                     qx_scratch[:, part, :].rearrange("(g r) c -> r g c", g=QUADS)).then_inc(qx_slots_in, 16)
                if r.early:
                    sp.wait_ge(qk_copied, r.w)
                    if r.n:
                        sp.wait_ge(rope_sin, r.n)
                    for half in range(2):
                        sp.dma_start(qk_swapped[half:P:2, :, :], qk[1 - half:P:2, :, :]).then_inc(qk_swap_in, 16)
                if r.last:
                    fixed_wait(sp)
                    sp.wait_ge(y_done, r.u)
                    sp.dma_start(out_d[r.e - 3].rearrange("(t p) d -> p t d", p=P), y[:]).then_inc(stored, 16)

            iterations(sp, "sp", "w n s m m_16 t t_48 u", body)
            sp.wait_ge(stored, 16 * (B + 1))

        @block.tensor
        def _(pe):
            ident = const("ident")
            sp_r, kd_r = slots[:].bitcast(F32R), k_diag[:].bitcast(F32R)
            qxs_r, kxd_r = qx_slots[:].bitcast(F32R), kx_diag[:].bitcast(F32R)
            mask_r, keys_r = mask_parts[:].bitcast(F32R), key_of_row[:].bitcast(F32R)

            def max_scores(g, t, done, free, free_count):
                pe.wait_ge(diag_done[g], done)
                if free_count:
                    pe.wait_ge(free, free_count)
                for h in range(0, HQ, 2):
                    mm = pe.matmul(scores_qk[:, h * S:(h + 2) * S], sp_r[0:NROWS, g, 0, t * P:(t + 1) * P],
                                   kd_r[0:NROWS, g, h:h + 2, :], start=True, stop=True)
                mm.then_inc(max_ready[g][t], 1)

            def exp_scores(g, half, done, free, free_count):
                if half == 0:
                    pe.wait_ge(maxT_in[g], done)
                if free_count:
                    pe.wait_ge(free, free_count)
                for j in range(2):
                    for kt in range(QT):
                        mm = pe.matmul(scores_kq[:, (2 * j + kt) * S:(2 * j + kt + 1) * S],
                                       kd_r[:, g, 2 * half + j, kt * P:(kt + 1) * P], sp_r[:, g, 0, :],
                                       start=True, stop=True)
                mm.then_inc(exp_ready[g][half], 1)

            def max_transposes(g, done):
                pe.wait_ge(max_split[g], done)
                pe.transpose(prep_ps[:, 0:P], max_parts[:, g, :, :], ident).then_inc(maxT_made[g], 1)

            def pv(g, done, previous):
                pe.wait_ge(exp_done[g][0], done)
                pe.wait_ge(exp_done[g][1], done)
                if g == 0:
                    pe.wait_ge(v_placed, done)
                    if previous:
                        pe.wait_ge(pv_copied[1], previous)
                if g == 2:
                    pe.wait_ge(pv_copied[0], done)
                for kt in range(QT):
                    for h in range(HQ):
                        mm = pe.matmul(pv_acc[STRIP * h:STRIP * (h + 1), g % 2, :], v_ones[:, kt, HQ * g + h, :],
                                       probs[:, g % 2, h, kt, :], start=(kt == 0), stop=(kt == QT - 1),
                                       tile_position=(0, STRIP * h))
                mm.then_inc(pv_done[g], 1)

            def maxx_scores(t, r):
                if t == 0:
                    if r.t:
                        pe.wait_ge(kx_diag_done, r.t)
                    if r.t:
                        pe.wait_ge(qx_slots_in, r.t_48)
                    if r.self_:
                        pe.wait_ge(max_done[1][1], r.s)
                    else:
                        pe.wait_ge(max_done[3][1], B)
                        pe.wait_ge(maxx_done[1], r.u)
                else:
                    if r.t:
                        pe.wait_ge(maxx_done[0], r.t)
                for half in range(2):
                    pe.matmul(scores_qk[:, half * 512:(half + 1) * 512], mask_r[:, t * P:(t + 1) * P], keys_r,
                              start=True, stop=False, skip_group_check=True)
                    for g in range(2 * half, 2 * half + 2):
                        mm = pe.matmul(scores_qk[:, g * 256:(g + 1) * 256], qxs_r[0:NROWS, g, t * P:(t + 1) * P],
                                       kxd_r[0:NROWS, g, :, :], start=False, stop=True, skip_group_check=True)
                mm.then_inc(maxx_ready[t], 1)

            def expx_scores(u, r):
                if u == 0:
                    if r.t:
                        pe.wait_ge(maxxT_in, r.t)
                    if r.self_:
                        pe.wait_ge(exp_done[1][1], r.s)
                    else:
                        pe.wait_ge(exp_done[3][1], B)
                        pe.wait_ge(expx_done[1], r.u)
                else:
                    if r.t:
                        pe.wait_ge(expx_done[0], r.t)
                for p in range(4 * u, 4 * u + 4):
                    o = scores_kq[:, (p % 4) * S:(p % 4 + 1) * S]
                    pe.matmul(o, keys_r[:, 0:P], mask_r, start=True, stop=False)
                    mm = pe.matmul(o, kxd_r[:, p // 2, 2 * (p % 2):2 * (p % 2) + 2, :], qxs_r[:, p // 2, :],
                                   start=False, stop=True)
                mm.then_inc(expx_ready[u], 1)

            def body(r):
                if r.starts_self:
                    pe.wait_ge(mask_step, 1)
                if r.starts_mid:
                    pe.wait_ge(later_in, 16)
                    pe.wait_ge(consts_ready, 1)
                if r.self_:
                    max_scores(1, 0, r.s, max_done[0][1], r.s)
                    pe.wait_ge(qk_copied, r.n)
                    if not r.early:
                        pe.wait_ge(maxT_in[3], r.m)
                    max_transposes(0, r.s)
                if r.last:
                    pe.wait_ge(att2_done, r.u)
                    for t in range(QT):
                        mm = pe.transpose(tail_ps[:, 0, t * P:(t + 1) * P], att2[:, t, :], ident)
                    mm.then_inc(att2T_made, 1)
                if r.mid:
                    pv(2, r.m, r.t)
                    exp_scores(3, 1, r.m, exp_done[3][0], r.m)
                if r.self_:
                    max_scores(1, 1, r.s, max_done[1][0], r.s)
                if r.tail:
                    if r.self_:
                        pe.wait_ge(maxT_in[0], r.s)
                    else:
                        pe.wait_ge(maxT_in[3], B)
                        pe.wait_ge(kx_copied, r.t)
                    pe.matmul(prep_ps[:, P:2 * P], ctxT2[:], const("wvx"), start=True, stop=True).then_inc(vx_made, 1)
                if r.last:
                    pe.wait_ge(att2T_copied, r.u)
                    for t in range(QT):
                        mm = pe.matmul(tail_ps[:, 1, t * P:(t + 1) * P], att2T[:, t * P:(t + 1) * P], const("dense"),
                                       start=True, stop=True)
                    mm.then_inc(dense_made, 1)
                if r.self_:
                    exp_scores(0, 0, r.s, exp_done[3][1], r.m)
                if r.tail:
                    maxx_scores(0, r)
                if r.mid:
                    pv(3, r.m, r.t)
                if r.self_:
                    if r.tail:
                        pe.wait_ge(vx_copied, r.t)
                    else:
                        pe.wait_ge(maxT_in[0], r.s)
                    max_transposes(1, r.s)
                    exp_scores(0, 1, r.s, exp_done[0][0], r.s)
                if r.tail:
                    maxx_scores(1, r)
                if r.mid:
                    pe.wait_ge(ctx_loaded, r.m_32)
                    if r.self_:
                        pe.wait_ge(maxT_in[1], r.s)
                    else:
                        pe.wait_ge(vx_copied, r.t)
                    pe.transpose(prep_ps[:, 0:P], ctx_in[:], ident).then_inc(ctxT_made, 1)
                    pe.wait_ge(pv_copied[1], r.m)
                    if r.u:
                        pe.wait_ge(sum2_done, r.u)
                    for t in range(QT):
                        for g in range(QUADS):
                            mm = pe.transpose(tail_ps[:, t, g * P:(g + 1) * P], ctxvT[:, g, t * P:(t + 1) * P], ident)
                    mm.then_inc(pvT_made, 1)
                if r.self_:
                    exp_scores(1, 0, r.s, exp_done[0][1], r.s)
                if r.self_:
                    if r.tail:
                        pe.wait_ge(maxx_done[1], r.t)
                    max_scores(2, 0, r.s, max_done[1][1], r.s)
                    pv(0, r.s, r.m)
                if r.last:
                    pe.wait_ge(x2_done, r.u)
                    if r.mid:
                        pe.wait_ge(att1_done, r.m)
                    for t in range(QT):
                        mm = pe.transpose(tail_ps[:, 0, t * P:(t + 1) * P], x2[:, t, :], ident)
                    mm.then_inc(x2T_made, 1)
                if r.tail:
                    pe.wait_ge(maxx_split, r.t)
                    if r.mid:
                        pe.wait_ge(ctxT_copied, r.m)
                    else:
                        pe.wait_ge(vx_copied, r.t)
                    for t in range(QT):
                        mm = pe.transpose(prep_ps[:, t * P:(t + 1) * P],
                                          maxx_parts[:, t * QUADS:(t + 1) * QUADS, :], ident)
                    mm.then_inc(maxxT_made, 1)
                if r.self_:
                    exp_scores(1, 1, r.s, exp_done[1][0], r.s)
                if r.self_:
                    max_scores(2, 1, r.s, max_done[2][0], r.s)
                if r.last:
                    pe.wait_ge(x2T_copied, r.u)
                    for c in range(FC):
                        mm = pe.matmul(tail_ps[:, c // 2, (c % 2) * S:(c % 2 + 1) * S], const("w1")[:, c * P:(c + 1) * P],
                                       x2T[:], start=True, stop=True)
                    mm.then_inc(h_made, 1)
                if r.mid:
                    pe.wait_ge(ctxT_copied, r.m)
                    if r.tail:
                        pe.wait_ge(maxxT_in, r.t)
                    pe.matmul(prep_ps[:, 0:SC], const("wkx"), ctxT2[:, 0:SC], start=True, stop=True).then_inc(kx_made, 1)
                if r.tail:
                    expx_scores(0, r)
                if r.self_:
                    max_scores(3, 0, r.s, max_done[2][1], r.s)
                    pv(1, r.s, r.m)
                    if r.mid:
                        pe.wait_ge(kx_copied, r.m)
                    else:
                        pe.wait_ge(maxT_in[1], r.s)
                    max_transposes(2, r.s)
                if r.tail:
                    expx_scores(1, r)
                if r.self_:
                    max_scores(3, 1, r.s, max_done[3][0], r.s)
                if r.mid:
                    pe.wait_ge(x1_done, r.m)
                    if r.last:
                        pe.wait_ge(h_copied, r.u)
                    for t in range(QT):
                        mm = pe.transpose(tail_ps[:, 0, t * P:(t + 1) * P], x1[:, t, :], ident)
                    mm.then_inc(x1T_made, 1)
                if r.last:
                    pe.wait_ge(h_copied, r.u)
                    for t in range(QT):
                        for c in range(FC):
                            mm = pe.matmul(tail_ps[:, 1, t * P:(t + 1) * P], hT[:, c, t * P:(t + 1) * P],
                                           const("w2")[:, c * D:(c + 1) * D], start=(c == 0), stop=(c == FC - 1))
                    mm.then_inc(ffn_made, 1)
                if r.self_:
                    if r.tail:
                        pe.wait_ge(expx_done[1], r.t)
                    exp_scores(2, 0, r.s, exp_done[1][1], r.s)
                if r.prep:
                    if r.self_:
                        pe.wait_ge(maxT_in[2], r.s)
                    else:
                        pe.wait_ge(second_in, 16)
                        pe.wait_ge(qk_copied, r.n)
                    for t in range(QT):
                        mm = pe.matmul(prep_ps[:, t * P:(t + 1) * P], xT[:, t * P:(t + 1) * P], const("wv"),
                                       start=True, stop=True)
                    mm.then_inc(v_made, 1)
                if r.prep:
                    max_scores(0, 0, r.n, max_done[3][1], r.s)
                if r.mid:
                    pe.wait_ge(x1T_copied, r.m)
                    pe.matmul(tail_ps[:, 0, S:2 * S], const("wqx"), x1T[:], start=True, stop=True).then_inc(qx_made, 1)
                if r.self_:
                    if r.prep:
                        pe.wait_ge(v_copied, r.n)
                    else:
                        pe.wait_ge(maxT_in[2], r.s)
                    max_transposes(3, r.s)
                    exp_scores(2, 1, r.s, exp_done[2][0], r.s)
                if r.tail:
                    pe.wait_ge(expx_done[0], r.t)
                    pe.wait_ge(expx_done[1], r.t)
                    pe.wait_ge(vx_copied, r.t)
                    if r.mid:
                        pe.wait_ge(qx_copied, r.m)
                    for p in range(PAIRS):
                        h = p % HQ
                        mm = pe.matmul(tail_ps[STRIP * h:STRIP * (h + 1), 0, (p // HQ) * S:(p // HQ + 1) * S],
                                       vx_ones[:, p, :], probsx[:, p, :], start=True, stop=True,
                                       tile_position=(0, STRIP * h))
                    mm.then_inc(pvx_done, 1)
                if r.early:
                    pe.wait_ge(x_loaded, r.w_16)
                    if r.self_:
                        pe.wait_ge(maxT_in[3], r.s)
                    elif r.prep:
                        pe.wait_ge(v_copied, r.n)
                    for t in range(QT):
                        mm = pe.transpose(prep_ps[:, t * P:(t + 1) * P], x_in[:, t, :], ident)
                    mm.then_inc(xT_made, 1)
                if r.prep:
                    max_scores(0, 1, r.n, max_done[0][0], r.n)
                if r.tail:
                    pe.wait_ge(pvx_copied, r.t)
                    if r.last:
                        pe.wait_ge(sum3_done, r.u)
                    for t in range(QT):
                        for j in range(2):
                            mm = pe.transpose(tail_ps[:, 1, (2 * t + j) * P:(2 * t + j + 1) * P],
                                              attvT[:, j, t * P:(t + 1) * P], ident)
                    mm.then_inc(pvxT_made, 1)
                if r.early:
                    pe.wait_ge(xT_copied, r.w)
                    pe.matmul(prep_ps[:, 0:S], const("wq"), xT[:], start=True, stop=True)
                    pe.matmul(prep_ps[:, S:2 * S], const("wk"), xT[:], start=True, stop=True).then_inc(qk_made, 1)
                if r.self_:
                    exp_scores(3, 0, r.s, exp_done[2][1], r.s)

            pe.wait_ge(first_in, 16)
            iterations(pe, "pe", "w w_16 n s m m_32 t t_48 u", body)

        @block.scalar
        def _(act):
            def exp(g, half, done, previous):
                act.wait_ge(exp_ready[g][half], done)
                if half == 0:
                    used = done if g >= 2 else previous
                    if used:
                        act.wait_ge(pv_done[(g + 2) % QUADS], used)
                nc.scalar.activation(probs[:, g % 2, 2 * half:2 * half + 2, :, :], scores_kq[:], ACT.Exp
                                     ).then_inc(exp_done[g][half], 1)

            def maxT(g, done):
                act.wait_ge(maxT_made[g], done)
                for t in range(QT):
                    ins = nc.scalar.copy(slots[NROWS:NROWS + MROWS, g, 0, t * P:(t + 1) * P].bitcast(F32R),
                                         prep_ps[t * P // QT:t * P // QT + MROWS, 0:P])
                ins.then_inc(maxT_in[g], 1)

            def pv_copy(half, done, previous):
                act.wait_ge(pv_done[2 * half + 1], done)
                if previous:
                    act.wait_ge(pvT_made, previous)
                nc.scalar.copy(ctxvT[:, 2 * half:2 * half + 2, :], pv_acc[:]).then_inc(pv_copied[half], 1)

            def body(r):
                if r.starts_self:
                    act.wait_ge(zeroed, 3)
                if r.starts_mid:
                    act.wait_ge(later_in, 16)
                if r.self_:
                    maxT(0, r.s)
                if r.last:
                    act.wait_ge(att2T_made, r.u)
                    nc.scalar.copy(att2T[:], tail_ps[:, 0, 0:S]).then_inc(att2T_copied, 1)
                if r.mid:
                    exp(3, 1, r.m, r.t)
                if r.self_:
                    exp(0, 0, r.s, r.m)
                if r.mid:
                    pv_copy(1, r.m, r.t)
                if r.self_:
                    maxT(1, r.s)
                    exp(0, 1, r.s, r.m)
                if r.mid:
                    act.wait_ge(ctxT_made, r.m)
                    if r.t:
                        act.wait_ge(vx_made, r.t)
                    nc.scalar.copy(ctxT2[:], prep_ps[:, 0:P]).then_inc(ctxT_copied, 1)
                if r.self_:
                    exp(1, 0, r.s, r.m)
                if r.last:
                    act.wait_ge(x2T_made, r.u)
                    nc.scalar.copy(x2T[:], tail_ps[:, 0, 0:S]).then_inc(x2T_copied, 1)
                if r.tail:
                    act.wait_ge(maxxT_made, r.t)
                    for g in range(QUADS):
                        ins = nc.scalar.copy(qx_slots[NROWS:NROWS + MROWS, g, :].bitcast(F32R),
                                             prep_ps[STRIP * g:STRIP * g + MROWS, 0:S])
                    ins.then_inc(maxxT_in, 1)
                if r.self_:
                    exp(1, 1, r.s, r.m)
                if r.last:
                    act.wait_ge(h_made, r.u)
                    for c in range(FC):
                        ins = nc.scalar.activation(hT[:, c, :], tail_ps[:, c // 2, (c % 2) * S:(c % 2 + 1) * S],
                                                   ACT.Relu, bias=const("b1")[:, c:c + 1])
                    ins.then_inc(h_copied, 1)
                if r.tail:
                    act.wait_ge(expx_ready[0], r.t)
                    nc.scalar.activation(probsx[:, 0:4, :], scores_kq[:], ACT.Exp).then_inc(expx_done[0], 1)
                if r.self_:
                    pv_copy(0, r.s, r.m)
                    maxT(2, r.s)
                if r.tail:
                    act.wait_ge(expx_ready[1], r.t)
                    nc.scalar.activation(probsx[:, 4:8, :], scores_kq[:], ACT.Exp).then_inc(expx_done[1], 1)
                if r.mid:
                    act.wait_ge(x1T_made, r.m)
                    nc.scalar.copy(x1T[:], tail_ps[:, 0, 0:S]).then_inc(x1T_copied, 1)
                if r.self_:
                    exp(2, 0, r.s, r.m)
                if r.mid:
                    act.wait_ge(qx_made, r.m)
                    if r.t:
                        act.wait_ge(qx_lo_done, r.t)
                    nc.scalar.activation(qx[:], tail_ps[:, 0, S:2 * S], ACT.Identity, bias=const("bqx")).then_inc(qx_copied, 1)
                if r.self_:
                    maxT(3, r.s)
                    exp(2, 1, r.s, r.m)
                if r.tail:
                    act.wait_ge(pvx_done, r.t)
                    if r.u:
                        act.wait_ge(pvxT_made, r.u)
                    nc.scalar.copy(attvT[:], tail_ps[:, 0, :]).then_inc(pvx_copied, 1)
                if r.early:
                    act.wait_ge(xT_made, r.w)
                    if r.n:
                        act.wait_ge(v_made, r.n)
                    nc.scalar.copy(xT[:], prep_ps[:, 0:S]).then_inc(xT_copied, 1)
                if r.early:
                    act.wait_ge(qk_made, r.w)
                    if r.n:
                        act.wait_ge(rope_cos, r.n)
                        act.wait_ge(qk_swap_in, r.n_32)
                    nc.scalar.activation(qk[:, 0, :], prep_ps[:, 0:S], ACT.Identity, bias=const("bq"))
                    nc.scalar.activation(qk[:, 1, :], prep_ps[:, S:2 * S], ACT.Identity, bias=const("bk")).then_inc(qk_copied, 1)
                if r.self_:
                    exp(3, 0, r.s, r.m)

            act.wait_ge(first_in, 16)
            iterations(act, "act", "w n n_32 s m t u", body)

        @block.vector
        def _(dve):
            nc.vector.memset(slots[NROWS:P, :, 0, :], 0.0)
            nc.vector.memset(slots[NROWS:P, :, 1, :], 1.0)
            nc.vector.memset(qx_slots[NROWS:P, :, :], 0.0)
            nc.vector.memset(kx_slots[NROWS:P, :, :], 1.0)
            nc.vector.memset(minus_half[:], -0.5)
            nc.vector.memset(y[:], 0.0).then_inc(stored, 16)
            nc.vector.memset(max_parts[:], 0.0)
            nc.vector.memset(maxx_parts[:], 0.0).then_inc(zeroed, 1)
            nc.vector.memset(v_ones[:], 0.0).then_inc(zeroed, 1)
            nc.vector.memset(vx_ones[:], 0.0).then_inc(zeroed, 1)
            dve.wait_ge(zeroed, 3)
            nc.vector.memset(v_ones[:, :, :, HD:HD + 1], 1.0).then_inc(mask_step, 1)
            nc.vector.memset(vx_ones[0:SC, :, HD:HD + 1], 1.0)
            nc.vector.memset(vx_ones[SC:P, :, 16 + HD:16 + HD + 1], 1.0)

            def reduce(g, t, done):
                dve.wait_ge(max_ready[g][t], done)
                nc.vector.tensor_reduce(neg_max[:, g, t, :], scores_qk[:].rearrange("p (h k) -> p h k", k=S), AX.X,
                                        ALU.max, negate=True).then_inc(max_done[g][t], 1)

            def split_max(g, done):
                dve.wait_ge(max_done[g][1], done)
                nc.vector.tensor_copy(max_parts[:, g, :, 0:HQ].bitcast(F32R), neg_max[:, g, :, :]).then_inc(max_hi_done[g], 1)
                dve.wait_ge(max_hi_done[g], done)
                nc.vector.tensor_tensor(max_parts[:, g, :, HQ:MROWS].bitcast(F32R), neg_max[:, g, :, :],
                                        max_parts[:, g, :, 0:HQ], ALU.subtract).then_inc(max_split[g], 1)

            def norm_stats(n, src, src_done, done):
                dve.wait_ge(src_done, done)
                for t in range(QT):
                    ins = nc.vector.bn_stats(stats[:, n, t, :], src[:, t, :])
                ins.then_inc(stats_done[n], 1)
                fixed_wait(dve)
                dve.wait_ge(stats_done[n], done)
                for t in range(QT):
                    ins = nc.vector.bn_aggr(mean_var[:, n, t, :], stats[:, n, t, :])
                ins.then_inc(aggr_done[n], 1)
                dve.wait_ge(aggr_done[n], done)
                nc.vector.tensor_scalar(var_eps[:, n, :], mean_var[:, n, :, 1], EPS, None, ALU.add).then_inc(var_done[n], 1)

            def normalize(n, src, out, out_done, done):
                dve.wait_ge(rstd_done[n], done)
                for t in range(QT):
                    ins = nc.vector.tensor_scalar(out[:, t, :], src[:, t, :], mean_var[:, n, t, 0:1], rstd[:, n, t:t + 1],
                                                  ALU.subtract, ALU.mult)
                ins.then_inc(out_done, 1)

            def qk_high(r):
                dve.wait_ge(rope_done, r.n)
                for g in range(QUADS):
                    if r.s:
                        dve.wait_ge(slots_in[g], r.s_48)
                nc.vector.tensor_copy(qk_parts[:, 0:4:2, :].bitcast(F32R), qk_rope[:]).then_inc(qk_hi_done, 1)

            def body(r):
                if r.self_:
                    reduce(1, 0, r.s)
                if r.self_:
                    reduce(1, 1, r.s)
                    split_max(1, r.s)
                if r.tail:
                    dve.wait_ge(vx_made, r.t)
                    if r.u:
                        dve.wait_ge(pvx_done, r.u)
                    for j in range(2):
                        rows = slice(j * SC, (j + 1) * SC)
                        ins = nc.vector.tensor_tensor(
                            vx_ones[rows, :, 16 * j:16 * j + HD],
                            prep_ps[rows, P:2 * P].rearrange("p (a j c) -> p a j c", j=2, c=HD)[:, :, j, :],
                            const("bvx")[rows, :].rearrange("p (a j c) -> p a j c", j=2, c=HD)[:, :, j, :], ALU.add)
                    ins.then_inc(vx_copied, 1)
                if r.last:
                    dve.wait_ge(dense_made, r.u)
                    dve.wait_ge(x1b_done, r.u)
                    nc.vector.tensor_tensor(sum2[:], tail_ps[:, 1, 0:S].rearrange("p (t d) -> p t d", t=QT), x1_bias[:],
                                            ALU.add).then_inc(sum2_done, 1)
                if r.tail:
                    dve.wait_ge(maxx_ready[0], r.t)
                    nc.vector.tensor_reduce(neg_maxx[:, 0:QUADS, :], scores_qk[:].rearrange("p (h k) -> p h k", k=SC), AX.X,
                                            ALU.max, negate=True).then_inc(maxx_done[0], 1)
                if r.last:
                    norm_stats(1, sum2, sum2_done, r.u)
                if r.tail:
                    dve.wait_ge(maxx_ready[1], r.t)
                    nc.vector.tensor_reduce(neg_maxx[:, QUADS:2 * QUADS, :], scores_qk[:].rearrange("p (h k) -> p h k", k=SC),
                                            AX.X, ALU.max, negate=True).then_inc(maxx_done[1], 1)
                    dve.wait_ge(maxx_done[1], r.t)
                    if r.u:
                        dve.wait_ge(maxxT_made, r.u)
                    nc.vector.tensor_copy(maxx_parts[:, :, 0:HQ].bitcast(F32R), neg_maxx[:]).then_inc(maxx_hi_done, 1)
                    dve.wait_ge(maxx_hi_done, r.t)
                    nc.vector.tensor_tensor(maxx_parts[:, :, HQ:MROWS].bitcast(F32R), neg_maxx[:], maxx_parts[:, :, 0:HQ],
                                            ALU.subtract).then_inc(maxx_split, 1)
                if r.last:
                    normalize(1, sum2, x2, x2_done, r.u)
                if r.mid:
                    dve.wait_ge(pvT_made, r.m)
                    pvT = tail_ps[:].rearrange("p t (h c) -> p (t h) c", c=STRIP)
                    nc.vector.reciprocal(recip1[:], pvT[:, :, HD]).then_inc(recip1_done, 1)
                    dve.wait_ge(recip1_done, r.m)
                    nc.vector.tensor_tensor(att1[:].rearrange("p t (h c) -> p (t h) c", c=HD), pvT[:, :, 0:HD],
                                            recip1[:].rearrange("p (h o) -> p h o", o=1).to_broadcast([P, QT * H, HD]),
                                            ALU.mult).then_inc(att1_done, 1)
                if r.self_:
                    reduce(2, 0, r.s)
                if r.prep and not r.starts_prep:
                    qk_high(r)
                if r.mid:
                    dve.wait_ge(att1_done, r.m)
                    dve.wait_ge(xres_loaded, r.m_16)
                    nc.vector.tensor_tensor(sum1[:], att1[:], x_res[:], ALU.add).then_inc(sum1_done, 1)
                if r.self_:
                    reduce(2, 1, r.s)
                    split_max(2, r.s)
                if r.mid:
                    norm_stats(0, sum1, sum1_done, r.m)
                if r.mid:
                    dve.wait_ge(kx_made, r.m)
                    if r.t:
                        dve.wait_ge(kx_lo_done, r.t)
                    nc.vector.tensor_scalar(kx[:], prep_ps[:, 0:SC], const("bkx"), KSCALE, ALU.add, ALU.mult).then_inc(kx_copied, 1)
                    dve.wait_ge(kx_copied, r.m)
                    if r.t:
                        dve.wait_ge(kx_out, r.t_16)
                    nc.vector.tensor_copy(kx_parts[:, 0, :].bitcast(F32R), kx[:]).then_inc(kx_hi_done, 1)
                    dve.wait_ge(kx_hi_done, r.m)
                    nc.vector.tensor_tensor(kx_parts[:, 1, :].bitcast(F32R), kx[:], kx_parts[:, 0, :], ALU.subtract
                                            ).then_inc(kx_lo_done, 1)
                if r.self_:
                    reduce(3, 0, r.s)
                if r.mid:
                    if r.t:
                        dve.wait_ge(x1b_done, r.t)
                        dve.wait_ge(x1T_made, r.t)
                    normalize(0, sum1, x1, x1_done, r.m)
                if r.self_:
                    reduce(3, 1, r.s)
                    split_max(3, r.s)
                if r.prep:
                    dve.wait_ge(v_made, r.n)
                    if r.s:
                        dve.wait_ge(v_placed, r.s)
                    nc.vector.tensor_copy(v_rows[:], prep_ps[:, 0:S].rearrange("p (t d) -> p t d", t=QT)).then_inc(v_copied, 1)
                if r.starts_prep:
                    dve.wait_ge(later_in, 16)
                    nc.vector.tensor_copy(key_of_row[:].bitcast(F32R), const("key_of_row"))
                    nc.vector.tensor_scalar(mask_neg[:], const("mask"), MASK_SCALE, None, ALU.mult).then_inc(mask_step, 1)
                    dve.wait_ge(mask_step, 2)
                    nc.vector.tensor_copy(mask_hi[:].bitcast(F32R), mask_neg[:])
                    nc.vector.tensor_copy(mask_parts[0:SC, :].bitcast(F32R), mask_neg[0:SC, :]).then_inc(mask_step, 1)
                    dve.wait_ge(mask_step, 3)
                    nc.vector.tensor_tensor(mask_parts[SC:P, :].bitcast(F32R), mask_neg[SC:P, :], mask_hi[SC:P, :], ALU.subtract
                                            ).then_inc(consts_ready, 1)
                    dve.wait_ge(second_in, 16)
                    rope_cosine(dve, nc.vector, r)
                    rope_sine(dve, nc.vector, r)
                    rope_sum(dve, nc.vector, r)
                    qk_high(r)
                    qk_low(dve, nc.vector, r)
                    diagonal(dve, nc.vector, 0, r.n_48, r.s)
                if r.prep:
                    reduce(0, 0, r.n)
                if r.mid:
                    dve.wait_ge(qx_copied, r.m)
                    if r.t:
                        dve.wait_ge(qx_out, r.t_16)
                    nc.vector.tensor_copy(qx_parts[:, 0, :].bitcast(F32R), qx[:]).then_inc(qx_hi_done, 1)
                if r.last:
                    dve.wait_ge(ffn_made, r.u)
                    dve.wait_ge(x2b_done, r.u)
                    nc.vector.tensor_tensor(sum3[:], tail_ps[:, 1, 0:S].rearrange("p (t d) -> p t d", t=QT), x2_bias[:],
                                            ALU.add).then_inc(sum3_done, 1)
                    norm_stats(2, sum3, sum3_done, r.u)
                if r.prep:
                    reduce(0, 1, r.n)
                    split_max(0, r.n)
                if r.tail:
                    dve.wait_ge(pvxT_made, r.t)
                    pvxT = tail_ps[:, 1, :].rearrange("p (h c) -> p h c", c=16)
                    nc.vector.reciprocal(recip2[:], pvxT[:, :, HD]).then_inc(recip2_done, 1)
                    dve.wait_ge(recip2_done, r.t)
                    nc.vector.tensor_tensor(att2[:].rearrange("p t (h c) -> p (t h) c", c=HD), pvxT[:, :, 0:HD],
                                            recip2[:].rearrange("p (h o) -> p h o", o=1).to_broadcast([P, QT * H, HD]),
                                            ALU.mult).then_inc(att2_done, 1)
                if r.last:
                    dve.wait_ge(stored, r.u_16)
                    normalize(2, sum3, y, y_done, r.u)

            dve.wait_ge(first_in, 16)
            iterations(dve, "dve", "n n_32 n_48 s s_48 m m_16 t t_16 u u_16", body)

        @block.gpsimd
        def _(pool):
            def inverse_std(n, done):
                pool.wait_ge(var_done[n], done)
                nc.gpsimd.tensor_tensor(rstd[:, n, :], var_eps[:, n, :], minus_half[:], ALU.pow).then_inc(rstd_done[n], 1)

            def body(r):
                if r.starts_mid:
                    pool.wait_ge(later_in, 16)
                if r.prep and not r.starts_prep:
                    rope_cosine(pool, nc.gpsimd, r)
                if r.self_:
                    diagonal(pool, nc.gpsimd, 2, r.s_48, r.m)
                if r.prep and not r.starts_prep:
                    rope_sine(pool, nc.gpsimd, r)
                if r.self_:
                    pool.wait_ge(v_copied, r.s)
                    if r.m:
                        pool.wait_ge(pv_done[3], r.m)
                    for t in range(QT):
                        ins = nc.gpsimd.tensor_tensor(v_ones[:, t, :, 0:HD], v_rows[:, t, :].rearrange("p (h c) -> p h c", c=HD),
                                                      const("bv").rearrange("p (h c) -> p h c", c=HD), ALU.add)
                    ins.then_inc(v_placed, 1)
                if r.last:
                    inverse_std(1, r.u)
                if r.prep and not r.starts_prep:
                    rope_sum(pool, nc.gpsimd, r)
                if r.tail:
                    pool.wait_ge(x1_done, r.t)
                    if r.u:
                        pool.wait_ge(sum2_done, r.u)
                    nc.gpsimd.tensor_tensor(x1_bias[:], x1[:], const("dense_b").rearrange("p (o d) -> p o d", o=1)
                                            .to_broadcast([P, QT, D]), ALU.add).then_inc(x1b_done, 1)
                if r.self_:
                    diagonal(pool, nc.gpsimd, 3, r.s_48, r.m)
                if r.prep and not r.starts_prep:
                    qk_low(pool, nc.gpsimd, r)
                if r.mid:
                    inverse_std(0, r.m)
                if r.last:
                    pool.wait_ge(x2_done, r.u)
                    nc.gpsimd.tensor_tensor(x2_bias[:], x2[:], const("b2").rearrange("p (o d) -> p o d", o=1)
                                            .to_broadcast([P, QT, D]), ALU.add).then_inc(x2b_done, 1)
                if r.prep and not r.starts_prep:
                    diagonal(pool, nc.gpsimd, 0, r.n_48, r.s)
                if r.mid:
                    pool.wait_ge(qx_hi_done, r.m)
                    nc.gpsimd.tensor_tensor(qx_parts[:, 1, :].bitcast(F32R), qx[:], qx_parts[:, 0, :], ALU.subtract
                                            ).then_inc(qx_lo_done, 1)
                if r.prep:
                    diagonal(pool, nc.gpsimd, 1, r.n_48, r.s)
                if r.last:
                    inverse_std(2, r.u)
                if r.mid:
                    pool.wait_ge(kx_slots_in, r.m_48)
                    if r.t:
                        pool.wait_ge(expx_ready[1], r.t)
                    for g in range(QUADS):
                        ins = nc.gpsimd.tensor_tensor(kx_diag[:, g, :, :].bitcast(F32R),
                                                      kx_slots[:, g:g + 1, :].to_broadcast([P, HQ, SC]),
                                                      row_head.to_broadcast([P, HQ, SC]), ALU.mult)
                    ins.then_inc(kx_diag_done, 1)

            pool.wait_ge(second_in, 16)
            pool.wait_ge(zeroed, 3)
            iterations(pool, "pool", "n n_32 n_48 s s_48 m m_48 t u", body)


def shape_constants():
    import numpy as np

    row = np.arange(P)
    dim = row % HD
    inv = np.power(np.float32(10000.0), -2.0 * np.arange(HD // 2, dtype=np.float32) / np.float32(HD)).astype(np.float32)
    angle = (np.arange(S, dtype=np.float32)[None, :] * inv[dim // 2][:, None]).astype(np.float32)
    sign = np.where(dim % 2 == 0, -1.0, 1.0)[:, None]
    scale = np.array([1.0, KSCALE])[None, :, None]
    cos = (np.cos(angle.astype(np.float64))[:, None, :] * scale).reshape(P, 2 * S)
    sin = ((sign * np.sin(angle.astype(np.float64)))[:, None, :] * scale).reshape(P, 2 * S)
    head = np.where(row < NROWS, (row % QROWS) // HD, np.where(row < NROWS + MROWS, row % HQ, -1))
    return {
        "ident": np.eye(P, dtype=np.float32),
        "cos": cos.astype(np.float32),
        "sin": sin.astype(np.float32),
        "head_of_row": (head[:, None] == np.arange(HQ)[None, :]).astype(np.float32),
        "key_of_row": (row[:, None] % SC == np.arange(8 * SC)[None, :] % SC).astype(np.float32),
    }


def kernel(**inputs):
    import numpy as np
    import concourse.bacc as bacc
    from concourse.bass_utils import run_bass_kernel_spmd

    a = {k: np.asarray(v) for k, v in inputs.items()}
    column = lambda v: v.reshape(-1, P).T
    every_row = lambda v: np.broadcast_to(v[None, :], (P, v.shape[0]))
    maskT = a["mask_1x1xSxS2_fk1"][0, 0].T
    parts = dict(shape_constants())
    parts.update(
        wq=a["L0_attn_Wq"], wk=a["L0_attn_Wk"], wv=a["L0_attn_Wv"],
        bq=column(a["L0_attn_bq"]), bk=column(a["L0_attn_bk"]), bv=every_row(a["L0_attn_bv"]),
        wqx=a["L0_xattn_wq_w"].T, wkx=a["L0_xattn_wk_w"].T, wvx=a["L0_xattn_wv_w"].T, dense=a["L0_xattn_dense_w"].T,
        w1=a["L0_ffn_W1"], w2=a["L0_ffn_W2"].reshape(FC, P, D).transpose(1, 0, 2).reshape(P, FC * D),
        bqx=column(a["L0_xattn_wq_b"]), bkx=column(a["L0_xattn_wk_b"]), b1=column(a["L0_ffn_b1"]),
        bvx=every_row(a["L0_xattn_wv_b"]), dense_b=every_row(a["L0_xattn_dense_b"]), b2=every_row(a["L0_ffn_b2"]),
        mask=np.concatenate([maskT, maskT], axis=0),
    )
    arrays = {
        "x": np.ascontiguousarray(a["x"]),
        "ctx": np.ascontiguousarray(a["ctx_1024"]),
        "first": np.ascontiguousarray(np.concatenate([parts[n] for n, _ in FIRST], axis=1)),
        "second": np.ascontiguousarray(np.concatenate([parts[n] for n, _ in SECOND], axis=1)),
        "later": np.ascontiguousarray(np.concatenate([parts[n] for n, _ in LATER], axis=1)),
    }
    nc = bacc.Bacc("TRN2", target_bir_lowering=False, num_devices=1)
    args = [nc.dram_tensor(n, v.shape, mybir.dt.from_np(v.dtype), kind="ExternalInput").ap() for n, v in arrays.items()]
    out = nc.dram_tensor("out", (B, S, D), F32, kind="ExternalOutput").ap()
    build(nc, *args, out)
    return run_bass_kernel_spmd(nc, [arrays], core_ids=[0]).results[0]["out"]
```
